# Optimizing a Trainium2 kernel written in Bass

```python
import numpy as np
import jax
import jax.numpy as jnp

def _softmax(x, axis=-1):
    return jax.nn.softmax(x, axis=axis)

def _gelu(x):
    return jax.nn.gelu(x, approximate=True)

def _silu(x):
    return jax.nn.silu(x)

def _sigmoid(x):
    return jax.nn.sigmoid(x)

def _layernorm(x, axis=-1, eps=1e-05):
    m = jnp.mean(x, axis=axis, keepdims=True)
    v = jnp.var(x, axis=axis, keepdims=True)
    return (x - m) / jnp.sqrt(v + eps)

def _scatter_add(tgt, idx, src, axis=0):
    return tgt.at[idx].add(src)

def _segment_sum(src, seg, n):
    return jax.ops.segment_sum(src, seg, n)
kernel_name = 'mk_xattn_ffn_d2_seqx_r8_a384c8'

def setup_inputs(seed: int=0):
    np.random.seed(seed)
    _w = jnp.asarray

    def _rec_inputs():
        import jax
        import jax.numpy as jnp
        _rk = jax.random.key(seed)
        x = -0.0002928 + 1 * jax.random.normal(jax.random.fold_in(_rk, 1), (4, 256, 128), jnp.float32)
        _lenS = 256 - jax.random.randint(jax.random.fold_in(_rk, 7), (4,), 0, max(1, 256 // 4) + 1, jnp.int32)
        _lenS2 = 64 - jax.random.randint(jax.random.fold_in(_rk, 8), (4,), 0, max(1, 64 // 4) + 1, jnp.int32)
        _ctx_1024P = jax.random.normal(jax.random.fold_in(_rk, 11), (4, 16, 128), jnp.float32)
        _ctx_1024c = jax.random.dirichlet(jax.random.fold_in(_rk, 511), 0.3 * jnp.ones((16,), jnp.float32), (4, 64))
        _ctx_1024t = jnp.einsum('bsk,bkd->bsd', _ctx_1024c, _ctx_1024P)
        _ctx_1024t = _ctx_1024t * jax.lax.rsqrt(jnp.mean(jnp.square(_ctx_1024t)) + 1e-12) * 0.953939
        ctx_1024 = -1.39393e-06 + 0.999914 * (_ctx_1024t + 0.3 * jax.random.normal(jax.random.fold_in(_rk, 611), (4, 64, 128), jnp.float32))
        return (x, ctx_1024)
    x, ctx_1024 = _rec_inputs()

    def _L0_xattn_setup():
        import jax, jax.numpy as jnp
        import numpy as np
        B, S, T, E, H = (2, 256, 256, 128, 16)
        D = E // H
        key = jax.random.key(seed)
        ks = jax.random.split(key, 11)
        scale = 1.0 / np.sqrt(E)
        return {'query': jax.random.normal(ks[0], (B, S, E), jnp.float32), 'value': jax.random.normal(ks[1], (B, T, E), jnp.float32), 'key': jax.random.normal(ks[2], (B, T, E), jnp.float32), 'Wq': jax.random.normal(ks[3], (E, E), jnp.float32) * scale, 'bq': jnp.zeros((E,), jnp.float32), 'Wk': jax.random.normal(ks[4], (E, E), jnp.float32) * scale, 'bk': jnp.zeros((E,), jnp.float32), 'Wv': jax.random.normal(ks[5], (E, E), jnp.float32) * scale, 'bv': jnp.zeros((E,), jnp.float32), 'Wo': jax.random.normal(ks[6], (E, E), jnp.float32) * scale, 'bo': jnp.zeros((E,), jnp.float32)}
    _L0_xattn_all = _L0_xattn_setup()
    _L0_xattn_in = {k: v for k, v in _L0_xattn_all.items() if k in ('Wq', 'bq', 'Wk', 'bk', 'Wv', 'bv', 'Wo', 'bo')}
    del _L0_xattn_all

    def _L0_ffn_setup():
        import jax, jax.numpy as jnp
        import numpy as np
        E = 8
        K = 2
        D = 128
        H = 128
        B, T = (2, 128)
        key = jax.random.key(seed)
        ks = jax.random.split(key, 6)
        s = 0.02
        return {'x': jax.random.normal(ks[0], (B, T, D), dtype=jnp.float32), 'gate_w': jax.random.normal(ks[1], (E, D), dtype=jnp.float32) * s, 'lb_bias': jnp.zeros((E,), dtype=jnp.float32), 'w1': jax.random.normal(ks[2], (E, H, D), dtype=jnp.float32) * s, 'w2': jax.random.normal(ks[3], (E, D, H), dtype=jnp.float32) * s, 'cfc': jax.random.normal(ks[4], (H, D), dtype=jnp.float32) * s, 'cproj': jax.random.normal(ks[5], (D, H), dtype=jnp.float32) * s}
    _L0_ffn_all = _L0_ffn_setup()
    _L0_ffn_in = {k: v for k, v in _L0_ffn_all.items() if k in ('gate_w', 'lb_bias', 'w1', 'w2', 'cfc', 'cproj')}
    del _L0_ffn_all

    def _L1_xattn_setup():
        import jax, jax.numpy as jnp
        import numpy as np
        B, S, SC, E, H = (2, 256, 256, 128, 16)
        D = E // H
        EPS = 1e-06

        def _layernorm(x, g, b):
            m = jnp.mean(x, axis=-1, keepdims=True)
            v = jnp.mean((x - m) ** 2, axis=-1, keepdims=True)
            return (x - m) / jnp.sqrt(v + EPS) * g + b

        def _mha(xk, xv, xq, Wk, Wv, Wq, Wo, bo, masked):
            K = jnp.einsum('bse,hed->bhsd', xk, Wk)
            V = jnp.einsum('bse,hed->bhsd', xv, Wv)
            Q = jnp.einsum('bqe,hed->bhqd', xq, Wq)
            scores = jnp.einsum('bhqd,bhkd->bhqk', Q, K)
            sk = xk.shape[1]
            if masked:
                causal = jnp.triu(jnp.ones((xq.shape[1], sk), dtype=bool), k=1)
                scores = jnp.where(causal, -jnp.inf, scores)
            att = jax.nn.softmax(scores / jnp.sqrt(jnp.asarray(sk, scores.dtype)), axis=-1)
            out = jnp.einsum('bhqk,bhkd->bhqd', att, V)
            out = out.transpose(0, 2, 1, 3).reshape(out.shape[0], out.shape[2], -1)
            return jax.nn.relu(out @ Wo + bo)
        key = jax.random.key(seed)
        ks = jax.random.split(key, 16)
        w = lambda k, shape: jax.random.normal(k, shape, jnp.float32) * 0.02
        return {'inputs': jax.random.normal(ks[0], (B, S, E), jnp.float32), 'context_seq': jax.random.normal(ks[1], (B, SC, E), jnp.float32), 'Wk1': w(ks[2], (H, E, D)), 'Wv1': w(ks[3], (H, E, D)), 'Wq1': w(ks[4], (H, E, D)), 'Wo1': w(ks[5], (E, E)), 'bo1': jnp.zeros((E,), jnp.float32), 'Wk2': w(ks[6], (H, E, D)), 'Wv2': w(ks[7], (H, E, D)), 'Wq2': w(ks[8], (H, E, D)), 'Wo2': w(ks[9], (E, E)), 'bo2': jnp.zeros((E,), jnp.float32), 'Wf': w(ks[10], (E, E)), 'bf': jnp.zeros((E,), jnp.float32), 'g1': jnp.ones((E,), jnp.float32), 'b1': jnp.zeros((E,), jnp.float32), 'g2': jnp.ones((E,), jnp.float32), 'b2': jnp.zeros((E,), jnp.float32), 'g3': jnp.ones((E,), jnp.float32), 'b3': jnp.zeros((E,), jnp.float32)}
    _L1_xattn_all = _L1_xattn_setup()
    _L1_xattn_in = {k: v for k, v in _L1_xattn_all.items() if k in ('Wk1', 'Wv1', 'Wq1', 'Wo1', 'bo1', 'Wk2', 'Wv2', 'Wq2', 'Wo2', 'bo2', 'Wf', 'bf', 'g1', 'b1', 'g2', 'b2', 'g3', 'b3')}
    del _L1_xattn_all

    def _L1_ffn_setup():
        import jax, jax.numpy as jnp
        import numpy as np
        DIM = 128
        HID = 512
        E = 8
        TOPK = 2
        ALPHA = 2.0
        B, T = (1, 256)
        DOWN_SCALE = 0.01
        key = jax.random.key(seed)
        ks = jax.random.split(key, 8)
        s = 1.0 / np.sqrt(DIM)
        sh = 1.0 / np.sqrt(HID)
        return {'x': jax.random.normal(ks[0], (B, T, DIM), jnp.float32), 'w_router': jax.random.uniform(ks[1], (DIM, E), jnp.float32, -s, s), 'w_up': jax.random.uniform(ks[2], (E - 1, DIM, HID), jnp.float32, -s, s), 'w_gate': jax.random.uniform(ks[3], (E - 1, DIM, HID), jnp.float32, -s, s), 'w_down': jax.random.normal(ks[4], (E - 1, HID, DIM), jnp.float32) * DOWN_SCALE, 'ws_up': jax.random.uniform(ks[5], (DIM, HID), jnp.float32, -s, s), 'ws_gate': jax.random.uniform(ks[6], (DIM, HID), jnp.float32, -s, s), 'ws_down': jax.random.normal(ks[7], (HID, DIM), jnp.float32) * DOWN_SCALE}
    _L1_ffn_all = _L1_ffn_setup()
    _L1_ffn_in = {k: v for k, v in _L1_ffn_all.items() if k in ('w_router', 'w_up', 'w_gate', 'w_down', 'ws_up', 'ws_gate', 'ws_down')}
    del _L1_ffn_all
    return {'x': x, 'ctx_1024': ctx_1024, 'L0_xattn_Wq': _L0_xattn_in['Wq'], 'L0_xattn_bq': _L0_xattn_in['bq'], 'L0_xattn_Wk': _L0_xattn_in['Wk'], 'L0_xattn_bk': _L0_xattn_in['bk'], 'L0_xattn_Wv': _L0_xattn_in['Wv'], 'L0_xattn_bv': _L0_xattn_in['bv'], 'L0_xattn_Wo': _L0_xattn_in['Wo'], 'L0_xattn_bo': _L0_xattn_in['bo'], 'L0_ffn_gate_w': _L0_ffn_in['gate_w'], 'L0_ffn_lb_bias': _L0_ffn_in['lb_bias'], 'L0_ffn_w1': _L0_ffn_in['w1'], 'L0_ffn_w2': _L0_ffn_in['w2'], 'L0_ffn_cfc': _L0_ffn_in['cfc'], 'L0_ffn_cproj': _L0_ffn_in['cproj'], 'L1_xattn_Wk1': _L1_xattn_in['Wk1'], 'L1_xattn_Wv1': _L1_xattn_in['Wv1'], 'L1_xattn_Wq1': _L1_xattn_in['Wq1'], 'L1_xattn_Wo1': _L1_xattn_in['Wo1'], 'L1_xattn_bo1': _L1_xattn_in['bo1'], 'L1_xattn_Wk2': _L1_xattn_in['Wk2'], 'L1_xattn_Wv2': _L1_xattn_in['Wv2'], 'L1_xattn_Wq2': _L1_xattn_in['Wq2'], 'L1_xattn_Wo2': _L1_xattn_in['Wo2'], 'L1_xattn_bo2': _L1_xattn_in['bo2'], 'L1_xattn_Wf': _L1_xattn_in['Wf'], 'L1_xattn_bf': _L1_xattn_in['bf'], 'L1_xattn_g1': _L1_xattn_in['g1'], 'L1_xattn_b1': _L1_xattn_in['b1'], 'L1_xattn_g2': _L1_xattn_in['g2'], 'L1_xattn_b2': _L1_xattn_in['b2'], 'L1_xattn_g3': _L1_xattn_in['g3'], 'L1_xattn_b3': _L1_xattn_in['b3'], 'L1_ffn_w_router': _L1_ffn_in['w_router'], 'L1_ffn_w_up': _L1_ffn_in['w_up'], 'L1_ffn_w_gate': _L1_ffn_in['w_gate'], 'L1_ffn_w_down': _L1_ffn_in['w_down'], 'L1_ffn_ws_up': _L1_ffn_in['ws_up'], 'L1_ffn_ws_gate': _L1_ffn_in['ws_gate'], 'L1_ffn_ws_down': _L1_ffn_in['ws_down']}

def reference(x, ctx_1024, L0_xattn_Wq, L0_xattn_bq, L0_xattn_Wk, L0_xattn_bk, L0_xattn_Wv, L0_xattn_bv, L0_xattn_Wo, L0_xattn_bo, L0_ffn_gate_w, L0_ffn_lb_bias, L0_ffn_w1, L0_ffn_w2, L0_ffn_cfc, L0_ffn_cproj, L1_xattn_Wk1, L1_xattn_Wv1, L1_xattn_Wq1, L1_xattn_Wo1, L1_xattn_bo1, L1_xattn_Wk2, L1_xattn_Wv2, L1_xattn_Wq2, L1_xattn_Wo2, L1_xattn_bo2, L1_xattn_Wf, L1_xattn_bf, L1_xattn_g1, L1_xattn_b1, L1_xattn_g2, L1_xattn_b2, L1_xattn_g3, L1_xattn_b3, L1_ffn_w_router, L1_ffn_w_up, L1_ffn_w_gate, L1_ffn_w_down, L1_ffn_ws_up, L1_ffn_ws_gate, L1_ffn_ws_down):
    import jax
    import jax.numpy as jnp

    def _L0_xattn_ref(query, value, key, Wq, bq, Wk, bk, Wv, bv, Wo, bo):
        import jax, jax.numpy as jnp
        import numpy as np
        B, S, T, E, H = (2, 256, 256, 128, 16)
        D = E // H
        b, s, e = query.shape
        t = value.shape[1]
        q = query @ Wq.T + bq
        k = key @ Wk.T + bk
        v = value @ Wv.T + bv
        q = q.reshape(b, s, H, D).transpose(0, 2, 1, 3)
        k = k.reshape(b, t, H, D).transpose(0, 2, 1, 3)
        v = v.reshape(b, t, H, D).transpose(0, 2, 1, 3)
        A = jnp.einsum('bhsd,bhtd->bhst', q, k) / jnp.sqrt(jnp.float32(D))
        A = jax.nn.softmax(A, axis=-1)
        out = jnp.einsum('bhst,bhtd->bhsd', A, v)
        out = out.transpose(0, 2, 1, 3).reshape(b, s, e)
        return out @ Wo.T + bo

    def _L0_ffn_ref(x, gate_w, lb_bias, w1, w2, cfc, cproj):
        import jax, jax.numpy as jnp
        import numpy as np
        E = 8
        K = 2
        D = 128
        H = 128
        B, T = (2, 128)
        Bx, Tx, Dx = x.shape
        logits = jnp.einsum('btd,ed->bte', x, gate_w)
        _, idx = jax.lax.top_k(logits + lb_bias, K)
        sel_logits = jnp.take_along_axis(logits, idx, axis=-1)
        w = jax.nn.sigmoid(sel_logits)
        w = w / (jnp.sum(w, axis=-1, keepdims=True) + 1e-06)
        xf = x.reshape(-1, Dx)
        idxf = idx.reshape(-1, K)
        wf = w.reshape(-1, K)
        onehot = jax.nn.one_hot(idxf, E, dtype=wf.dtype)
        we = jnp.einsum('nke,nk->ne', onehot, wf)
        hidden = jnp.square(jax.nn.relu(jnp.einsum('nd,ehd->neh', xf, w1)))
        expert_out = jnp.einsum('neh,edh->ned', hidden, w2)
        moe_out = jnp.einsum('ned,ne->nd', expert_out, we).reshape(Bx, Tx, Dx)
        sh = jnp.square(jax.nn.relu(jnp.einsum('btd,hd->bth', x, cfc)))
        shared = jnp.einsum('bth,dh->btd', sh, cproj)
        return moe_out + shared

    def _L1_xattn_ref(inputs, context_seq, Wk1, Wv1, Wq1, Wo1, bo1, Wk2, Wv2, Wq2, Wo2, bo2, Wf, bf, g1, b1, g2, b2, g3, b3):
        import jax, jax.numpy as jnp
        import numpy as np
        B, S, SC, E, H = (2, 256, 256, 128, 16)
        D = E // H
        EPS = 1e-06

        def _layernorm(x, g, b):
            m = jnp.mean(x, axis=-1, keepdims=True)
            v = jnp.mean((x - m) ** 2, axis=-1, keepdims=True)
            return (x - m) / jnp.sqrt(v + EPS) * g + b

        def _mha(xk, xv, xq, Wk, Wv, Wq, Wo, bo, masked):
            K = jnp.einsum('bse,hed->bhsd', xk, Wk)
            V = jnp.einsum('bse,hed->bhsd', xv, Wv)
            Q = jnp.einsum('bqe,hed->bhqd', xq, Wq)
            scores = jnp.einsum('bhqd,bhkd->bhqk', Q, K)
            sk = xk.shape[1]
            if masked:
                causal = jnp.triu(jnp.ones((xq.shape[1], sk), dtype=bool), k=1)
                scores = jnp.where(causal, -jnp.inf, scores)
            att = jax.nn.softmax(scores / jnp.sqrt(jnp.asarray(sk, scores.dtype)), axis=-1)
            out = jnp.einsum('bhqk,bhkd->bhqd', att, V)
            out = out.transpose(0, 2, 1, 3).reshape(out.shape[0], out.shape[2], -1)
            return jax.nn.relu(out @ Wo + bo)
        a = _mha(inputs, inputs, inputs, Wk1, Wv1, Wq1, Wo1, bo1, masked=True)
        a = _layernorm(inputs + a, g1, b1)
        c = _mha(context_seq, context_seq, a, Wk2, Wv2, Wq2, Wo2, bo2, masked=False)
        c = _layernorm(c + c, g2, b2)
        f = jax.nn.relu(c @ Wf + bf)
        return _layernorm(c + f, g3, b3)

    def _L1_ffn_ref(x, w_router, w_up, w_gate, w_down, ws_up, ws_gate, ws_down):
        import jax, jax.numpy as jnp
        import numpy as np
        DIM = 128
        HID = 512
        E = 8
        TOPK = 2
        ALPHA = 2.0
        B, T = (1, 256)
        DOWN_SCALE = 0.01
        logits = x @ w_router
        probs = jax.nn.softmax(logits.astype(jnp.float32), axis=-1).astype(logits.dtype)
        topk_vals, topk_idx = jax.lax.top_k(probs, TOPK)
        up = jnp.einsum('btd,edh->ebth', x, w_up)
        gate = jax.nn.silu(jnp.einsum('btd,edh->ebth', x, w_gate))
        exp_out = jnp.einsum('ebth,ehd->ebtd', up * gate, w_down)
        out = jnp.zeros_like(x)
        eids = jnp.arange(E - 1)
        for i in range(TOPK - 1):
            idx_i = topk_idx[..., i]
            sel = (idx_i[None, :, :] == eids[:, None, None]).astype(x.dtype)
            gathered = jnp.einsum('ebt,ebtd->btd', sel, exp_out)
            out = out + ALPHA * topk_vals[..., i:i + 1] * gathered
        shared = x @ ws_up * jax.nn.silu(x @ ws_gate) @ ws_down
        return out + shared
    x = x + _L0_xattn_ref(_layernorm(x, axis=-1), ctx_1024, ctx_1024, L0_xattn_Wq, L0_xattn_bq, L0_xattn_Wk, L0_xattn_bk, L0_xattn_Wv, L0_xattn_bv, L0_xattn_Wo, L0_xattn_bo)
    x = x + _L0_ffn_ref(_layernorm(x, axis=-1), L0_ffn_gate_w, L0_ffn_lb_bias, L0_ffn_w1, L0_ffn_w2, L0_ffn_cfc, L0_ffn_cproj)
    x = x + _L1_xattn_ref(_layernorm(x, axis=-1), ctx_1024, L1_xattn_Wk1, L1_xattn_Wv1, L1_xattn_Wq1, L1_xattn_Wo1, L1_xattn_bo1, L1_xattn_Wk2, L1_xattn_Wv2, L1_xattn_Wq2, L1_xattn_Wo2, L1_xattn_bo2, L1_xattn_Wf, L1_xattn_bf, L1_xattn_g1, L1_xattn_b1, L1_xattn_g2, L1_xattn_b2, L1_xattn_g3, L1_xattn_b3)
    x = x + _L1_ffn_ref(_layernorm(x, axis=-1), L1_ffn_w_router, L1_ffn_w_up, L1_ffn_w_gate, L1_ffn_w_down, L1_ffn_ws_up, L1_ffn_ws_gate, L1_ffn_ws_down)
    return x

_drawn_inputs = setup_inputs


def setup_inputs(seed=0):
    import zlib

    import numpy as np

    out = dict(_drawn_inputs(seed))
    spreads = {'L0_xattn_bq': (0.0, 0.421),
     'L0_xattn_bk': (0.0, 2.0),
     'L0_xattn_bv': (0.0, 0.1),
     'L0_xattn_bo': (0.0, 0.1),
     'L0_ffn_lb_bias': (0.0, 0.8),
     'L1_xattn_bo1': (0.0, 2.0),
     'L1_xattn_bo2': (0.0, 0.1),
     'L1_xattn_bf': (0.0, 0.319),
     'L1_xattn_g1': (1.0, 0.6),
     'L1_xattn_b1': (0.0, 0.8),
     'L1_xattn_g2': (1.0, 0.2),
     'L1_xattn_b2': (0.0, 0.297),
     'L1_xattn_g3': (1.0, 0.2),
     'L1_xattn_b3': (0.0, 0.271)}
    factors = {'L0_ffn_gate_w': 8.0,
     'L0_ffn_w1': 8.0,
     'L0_ffn_w2': 8.0,
     'L0_ffn_cfc': 6.411,
     'L0_ffn_cproj': 5.697,
     'L1_xattn_Wk1': 33.075,
     'L1_xattn_Wv1': 8.0,
     'L1_xattn_Wq1': 32.575,
     'L1_xattn_Wo1': 8.0,
     'L1_xattn_Wk2': 8.0,
     'L1_xattn_Wq2': 8.0,
     'L1_ffn_w_router': 4.352,
     'L1_ffn_w_up': 4.357,
     'L1_ffn_w_gate': 4.44,
     'L1_ffn_w_down': 4.349,
     'L1_ffn_ws_up': 8.0,
     'L1_ffn_ws_gate': 8.0,
     'L1_ffn_ws_down': 8.0}
    for name, (base, spread) in spreads.items():
        noise = np.random.default_rng([zlib.crc32(name.encode()), seed]).standard_normal(out[name].shape)
        drawn = base * np.exp(spread * noise) if base else spread * noise
        out[name] = jnp.asarray(drawn.astype(out[name].dtype))
    for name, factor in factors.items():
        out[name] = (out[name] * factor).astype(out[name].dtype)
    return out
```

```python
from contextlib import ExitStack

import numpy as np
import concourse.bass as bass
import concourse.mybir as mybir

ALU = mybir.AluOpType
ACT = mybir.ActivationFunctionType
F32 = mybir.dt.float32
F32R = mybir.dt.float32r
U32 = mybir.dt.uint32
AX_X = mybir.AxisListType.X

P = 128
B, S, SC = 4, 256, 64
H, D = 16, 8
G, T = 2, 4
GT = T * P
QUADS, SLOT = 4, 32
E0 = 9
E1, HID, CH = 8, 512, 4
NEG = -1.0e30
DV = D + 1

ROWS = ["bv", "bo", "bo1", "g1", "b1", "bo2", "g2", "b2", "bf", "g3", "b3"]
STACKS = ["k0", "q0", "k1", "q1", "k2", "q2"]
SQUARE = ["v0", "o0", "v1", "o1", "v2", "o2", "f"]
CONST = {"ident": 0, "tri_q": 128, "tri_k": 256, "signs": 384, "iota": 390}
NCONST = 398


def schedule():
    ev = [("ctx",), ("bias",), ("vctx", 0)]
    ev += [("stack", "k0", 0, j) for j in range(QUADS)]
    for g in range(G):
        ev += [("ln_stats", "x0", g), ("ln_norm", "x0", g), ("turn", "x0", g)]
    for g in range(G):
        ev += [("stack", "q0", g, j) for j in range(QUADS)]

    def attention(a):
        nmax, nst = (12, 16) if a == 1 else (4, 4)
        out = []
        if a == 1:
            out += [("kblocks", a, 0)]
        out += [("max", a, 0, u) for u in range(nmax)] + [("negmax", a, 0)]
        for b in range(B):
            steps = [("scores", a, b, u) for u in range(nst)]
            nxt = []
            if b + 1 < B:
                if a == 1 and b == 1:
                    nxt += [("stack", "k1", 1, j) for j in range(QUADS)]
                if a == 1:
                    nxt += [("kblocks", a, b + 1)]
                nxt += [("max", a, b + 1, u) for u in range(nmax)] + [("negmax", a, b + 1)]
            done = 0
            for i, s in enumerate(steps):
                out.append(s)
                want = len(nxt) * (i + 1) // len(steps)
                out += nxt[done:want]
                done = want
                if i:
                    out.append(("pv", a, b, i - 1))
            out += [("pv", a, b, nst - 1), ("out_norm", a, b)]
            if b % 2:
                out += [("turn", f"o{a}", b // 2), ("square", f"o{a}", b // 2)]
        return out

    ev += attention(0)
    for g in range(G):
        ev += [("ln_stats", "x1", g), ("ln_norm", "x1", g), ("turn", "x1", g), ("gate0", g)]
    for g in range(G):
        ev += [("up0", g, e) for e in (0, 1)]
        for e in range(E0):
            ev += [("down0", g, e)]
            ev += [("up0", g, e + 2)] if e + 2 < E0 else []
    ev += [("vctx", 2)] + [("stack", "k2", 0, j) for j in range(QUADS)]
    for g in range(G):
        ev += [("ln_stats", "x2", g), ("ln_norm", "x2", g), ("turn", "x2", g), ("square", "v1", g)]
        ev += [("stack", "q1", g, j) for j in range(QUADS)]
        if g == 0:
            ev += [("stack", "k1", 0, j) for j in range(QUADS)]
    ev += attention(1)
    ev += [("wsplit", 0), ("wsplit", 1)]
    for g in range(G):
        ev += [("ln_stats", "a", g), ("ln_norm", "a", g), ("turn", "a", g)]
    for g in range(G):
        ev += [("stack", "q2", g, j) for j in range(QUADS)]
    ev += attention(2)
    for g in range(G):
        ev += [("ln_stats", "c", g), ("ln_norm", "c", g), ("turn", "c", g), ("square", "f", g)]
    for g in range(G):
        ev += [("ln_stats", "f", g), ("ln_norm", "f", g), ("ln_stats", "x3", g), ("ln_norm", "x3", g),
               ("turn", "x3", g), ("xsplit", g)]
    chunks = [(n, g, c) for n in range(E1) for g in range(G) for c in range(CH)]
    late = [("gate1", 0), ("gate1", 1)]
    for i, k in enumerate(chunks + [None, None]):
        if k:
            ev.append(("up1",) + k)
        if i >= 2:
            n, g, c = chunks[i - 2]
            ev.append(("down1", n, g, c))
            if c == CH - 1:
                if n == 0:
                    ev.append(late.pop(0))
                ev.append(("add1", n, g))
                if g == 1 and n + 2 < E1:
                    ev.append(("wsplit", n + 2))
    ev += [("store", g) for g in range(G)]
    return ev


def order(n):
    return (E1 - 1 + n) % E1


def build(nc, x, ctx, const, stacks, qkbias, squares, rows, gates, w0, w1, out):
    ev = schedule()
    nth, seen = {}, {}
    for e in ev:
        seen[e[0]] = seen.get(e[0], 0) + 1
        nth[e] = seen[e[0]]

    with ExitStack() as stk:
        def sb(name, shape, dt=F32):
            return stk.enter_context(nc.sbuf_tensor(name, shape, dt))

        def sem(name):
            return stk.enter_context(nc.semaphore(name))

        cst = sb("cst", [P, NCONST])
        identr = sb("identr", [P, P], F32R)
        pairsel = sb("pairsel", [P, H // 2, 2 * SC], F32R)
        trir = sb("trir", [P, 2, P], F32R)
        neghalf = sb("neghalf", [P, T])
        onesr = sb("onesr", [P, GT], F32R)
        braw = sb("braw", [P, 2, QUADS * P])
        bsl = sb("bsl", [P, 2, QUADS * P], F32R)
        ws = sb("ws", [P, len(STACKS), QUADS * P])
        wsq = sb("wsq", [P, len(SQUARE), P])
        rowb = sb("rowb", [P, len(ROWS) * P + 8])
        wg = sb("wg", [P, 2, 8])
        we0 = sb("we0", [P, 2, E0 * P])
        wraw = sb("wraw", [P, 2, 3 * HID])
        big = sb("big", [P, 9216], F32R)
        X = sb("X", [P, G, T, P])
        xb = sb("xb", [P, G, T, P])
        cx = sb("cx", [P, 2, P])
        cxT = sb("cxT", [P, B * SC])
        cxT2 = sb("cxT2", [P, B, 2, SC])
        stat = sb("stat", [P, T, 6])
        mv = sb("mv", [P, 7 * G, T, 2])
        rstd = sb("rstd", [P, 7 * G, T])
        lnx = sb("lnx", [P, G, T, P])
        lni = sb("lni", [P, G, T, P])
        act = sb("act", [P, G, T, P])
        o_n = sb("o_n", [P, G, T, P])
        tT = sb("tT", [P, G, 2, GT])
        QS = sb("QS", [P, G, QUADS, GT], F32R)
        KS = sb("KS", [P, QUADS, GT], F32R)
        T1 = sb("T1", [P, 2, GT], F32R)
        bhi = T1
        KBX = sb("KBX", [P, QUADS, B, 4, SC], F32R)
        VBX = sb("VBX", [P, 2, B, H // 2, 2 * DV])
        VS = sb("VS", [P, G, T, H, DV])
        MX = sb("MX", [P, 2, 2, H])
        MP = sb("MP", [P, 2, 2, P])
        MT = sb("MT", [P, 2, S], F32R)
        pr = sb("pr", [P, 4, GT])
        rec = sb("rec", [P, 2, H])
        lg = sb("lg", [P, T, 8])
        zz = sb("zz", [P, T, 8])
        ex = sb("ex", [P, T, 8])
        m8 = sb("m8", [P, T, 8])
        i8 = sb("i8", [P, T, 8], U32)
        i8f = sb("i8f", [P, T, 8])
        sel = sb("sel", [P, 2, T, 8])
        r1 = sb("r1", [P, T, 1])
        r2 = sb("r2", [P, T, 1])
        wt = sb("wt", [P, 2, G, T, 8])
        hr = sb("hr", [P, 3, GT])
        hh = pr
        hhi, hlo = QS[:, 0], QS[:, 1]
        XH, XL = KS[:, 0:2], KS[:, 2:4]

        ps = [stk.enter_context(nc.psum_tensor(f"ps{i}", [P, GT], F32)) for i in range(8)]

        in_ctx, in_cst, in_x = sem("in_ctx"), sem("in_cst"), sem("in_x")
        in_small, in_st = sem("in_small"), sem("in_st")
        in_w0, in_w1, out_done = sem("in_w0"), [sem("in_w1a"), sem("in_w1b")], sem("out_done")
        zeroed, xb_ready = sem("zeroed"), sem("xb_ready")
        const_ready, bias_rows, bias_ready = sem("const_ready"), sem("bias_rows"), sem("bias_ready")
        ctx_turned, ctx_ready = sem("ctx_turned"), sem("ctx_ready")
        vctx_mm, vctx_ready = sem("vctx_mm"), sem("vctx_ready")
        stack_mm, stack_high, stack_ready = sem("stack_mm"), sem("stack_high"), sem("stack_ready")
        ln_stat, ln_rstd, ln_done = sem("ln_stat"), sem("ln_rstd"), sem("ln_done")
        turn_mm, turn_ready = sem("turn_mm"), sem("turn_ready")
        kb_ready = sem("kb_ready")
        max_mm, max_read, neg_ready = sem("max_mm"), sem("max_read"), sem("neg_ready")
        neg_mm, negT_ready = sem("neg_mm"), sem("negT_ready")
        sc_mm, pr_ready, pv_done = sem("sc_mm"), sem("pr_ready"), sem("pv_done")
        o_ready = sem("o_ready")
        sq_mm, sq_read = sem("sq_mm"), sem("sq_read")
        g0_mm, g0_lg, g0_exp, g0_ready = sem("g0_mm"), sem("g0_lg"), sem("g0_exp"), sem("g0_ready")
        g1_mm, g1_sub, g1_exp, g1_ready = sem("g1_mm"), sem("g1_sub"), sem("g1_exp"), sem("g1_ready")
        up0_mm, relu_ready, h0_ready, dn0_mm, dn0_read = (sem("up0_mm"), sem("relu_ready"), sem("h0_ready"),
                                                          sem("dn0_mm"), sem("dn0_read"))
        w_ready, xs_ready = sem("w_ready"), sem("xs_ready")
        up1_mm, silu_ready, h1_ready, hi_ready, lo_ready = (sem("up1_mm"), sem("silu_ready"), sem("h1_ready"),
                                                            sem("hi_ready"), sem("lo_ready"))
        dn1_chunk, dn1_mm, dn1_read = sem("dn1_chunk"), sem("dn1_mm"), sem("dn1_read")
        dve_step, act_step, pool_step = sem("dve_step"), sem("act_step"), sem("pool_step")

        ident = cst[:, CONST["ident"]:CONST["ident"] + P]
        sign = {n: cst[:, CONST["signs"] + i:CONST["signs"] + i + 1]
                for i, n in enumerate(["qa", "qb", "ka", "kb", "ba", "bb"])}
        iota = cst[:, CONST["iota"]:CONST["iota"] + 8]
        kbs = [big[:, 4096 * i:4096 * (i + 1)].rearrange("p (j h k) -> p j h k", j=QUADS, h=4) for i in range(2)]

        def row(name):
            i = ROWS.index(name)
            return rowb[:, i * P:(i + 1) * P]

        def rows4(name):
            return row(name).unsqueeze(1).broadcast_to([P, T, P])

        def stack_w(name, j):
            return ws[:, STACKS.index(name), j * P:(j + 1) * P]

        def square_w(name):
            return wsq[:, SQUARE.index(name), :]

        def hi_lo(n, part, c):
            base = (n % 3) * 3072
            o = part * HID + c * P
            return big[:, base + o:base + o + P], big[:, base + 1536 + o:base + 1536 + o + P]

        LN = {"x0": (X, lnx, 1e-5, None), "x1": (X, lnx, 1e-5, None), "x2": (X, lni, 1e-5, None),
              "a": (act, lnx, 1e-6, ("g1", "b1")), "c": (act, lnx, 1e-6, ("g2", "b2")),
              "f": (act, act, 1e-6, ("g3", "b3")), "x3": (X, lnx, 1e-5, None)}
        TURN = {"x0": (lnx, 0), "o0": (o_n, 1), "x1": (lnx, 0), "x2": (lni, 0), "o1": (o_n, 1),
                "a": (lnx, 0), "o2": (o_n, 1), "c": (lnx, 0), "x3": (lnx, 0)}
        SCALE = [float(D) ** -0.5, float(S) ** -0.5, float(SC) ** -0.5]

        block = stk.enter_context(nc.Block())

        @block.sync
        def _(sp):
            sp.dma_start(cx[:], ctx.rearrange("(t p) d -> p t d", p=P)).then_inc(in_ctx, 16)
            sp.dma_start(cst[:], const).then_inc(in_cst, 16)
            sp.dma_start(X[:], x.rearrange("(g t p) d -> p g t d", g=G, p=P)).then_inc(in_x, 16)
            sp.dma_start(ws[:], stacks).then_inc(in_st, 16)
            sp.dma_start(rowb[:], rows.partition_broadcast(P)).then_inc(in_small, 16)
            sp.dma_start(wsq[:], squares).then_inc(in_small, 16)
            sp.dma_start(wg[:], gates).then_inc(in_small, 16)
            sp.wait_ge(zeroed, 2)
            for r in range(2):
                sp.dma_start(braw[r:r + 1, :, :], qkbias).then_inc(bias_rows, 16)
            sp.dma_start(we0[:], w0).then_inc(in_w0, 16)
            for n in range(E1):
                if n >= 2:
                    sp.wait_ge(w_ready, n - 1)
                sp.dma_start(wraw[:, n % 2, :], w1[:, order(n), :]).then_inc(in_w1[n % 2], 16)
            for e in ev:
                if e[0] == "store":
                    g = e[1]
                    sp.wait_ge(dn1_read, G * (E1 - 1) + g + 1)
                    sp.dma_start(out.rearrange("(g t p) d -> p g t d", g=G, p=P)[:, g], X[:, g]).then_inc(out_done, 16)
            sp.wait_ge(out_done, 16 * G)

        @block.gpsimd
        def _(pool):
            step = [0]

            def link(ins):
                step[0] += 1
                ins.then_inc(pool_step, 1)
                pool.wait_ge(pool_step, step[0])

            nc.gpsimd.memset(braw[:], 0.0).then_inc(zeroed, 1)
            nc.gpsimd.memset(neghalf[:], -0.5).then_inc(zeroed, 1)
            nc.gpsimd.memset(KBX[:].bitcast(F32), 0.0).then_inc(zeroed, 1)
            nc.gpsimd.memset(VBX[:], 0.0).then_inc(zeroed, 1)
            nc.gpsimd.memset(MP[:], 0.0).then_inc(zeroed, 1)
            nc.gpsimd.memset(VS[:, :, :, :, D:DV], 1.0).then_inc(zeroed, 1)
            pool.wait_ge(zeroed, 6)
            nc.gpsimd.memset(VBX[0:64, :, :, :, D:DV], 1.0).then_inc(zeroed, 1)
            pool.wait_ge(zeroed, 7)
            nc.gpsimd.memset(VBX[64:128, :, :, :, D + DV:2 * DV], 1.0).then_inc(zeroed, 1)
            pool.wait_ge(zeroed, 8)
            nc.gpsimd.memset(big[:, 0:8192].bitcast(F32), 0.0).then_inc(zeroed, 1)
            pool.wait_ge(in_x, 16)
            pool.wait_ge(in_small, 48)
            for g in range(G):
                nc.gpsimd.tensor_tensor(xb[:, g], X[:, g], rows4("bo"), ALU.add).then_inc(xb_ready, 1)
            for e in ev:
                if e[0] == "ln_stats":
                    k = nth[e] - 1
                    pool.wait_ge(ln_stat, k + 1)
                    link(nc.gpsimd.tensor_scalar(rstd[:, k, :], mv[:, k, :, 1], LN[e[1]][2], None, ALU.add))
                    nc.gpsimd.tensor_tensor(rstd[:, k, :], rstd[:, k, :], neghalf[:], ALU.pow).then_inc(ln_rstd, 1)
                elif e[0] == "wsplit":
                    n = e[1]
                    pool.wait_ge(in_w1[n % 2], 16 * (n // 2 + 1))
                    if n < 2:
                        pool.wait_ge(pv_done, 4 * B + 16 * B)
                    elif n >= 3:
                        pool.wait_ge(dn1_mm, G * (n - 2))
                    base = (n % 3) * 3072
                    hi, lo = big[:, base:base + 1536], big[:, base + 1536:base + 3072]
                    link(nc.gpsimd.tensor_copy(hi, wraw[:, n % 2, :]))
                    nc.gpsimd.tensor_tensor(lo, wraw[:, n % 2, :], hi.bitcast(F32), ALU.subtract).then_inc(w_ready, 1)

        @block.tensor
        def _(pe):
            emptied = {}

            def take(bank, read_signal, value):
                if bank in emptied:
                    pe.wait_ge(*emptied[bank])
                emptied[bank] = (read_signal, value)

            pe.wait_ge(in_cst, 16)
            for e in ev:
                kind, n = e[0], nth[e]
                if kind == "ctx":
                    pe.wait_ge(in_ctx, 16)
                    take(5, ctx_ready, 1)
                    for t in range(2):
                        mm = nc.tensor.transpose(ps[5][:, t * P:(t + 1) * P], cx[:, t, :], ident)
                    mm.then_inc(ctx_turned, 1)
                elif kind == "vctx":
                    if n == 1:
                        pe.wait_ge(ctx_ready, 2)
                        pe.wait_ge(in_small, 48)
                    take(4, vctx_ready, n)
                    for b in range(B):
                        mm = nc.tensor.matmul(ps[4][:, b * P:(b + 1) * P], cxT2[:, b, :, :].rearrange("p a k -> p (a k)"),
                                              square_w(f"v{e[1]}"), start=True, stop=True)
                    mm.then_inc(vctx_mm, 1)
                elif kind == "stack":
                    _, name, g, j = e
                    bank = 6 + n % 2
                    if n == 1:
                        pe.wait_ge(in_st, 16)
                        pe.wait_ge(bias_ready, 1)
                    if name in ("k0", "k2"):
                        src, width = cxT[:], B * SC
                    else:
                        src, width = tT[:, g, 0, :], GT
                        if j == 0:
                            pe.wait_ge(turn_ready, nth[("turn", {"q0": "x0", "q1": "x2", "k1": "x2", "q2": "a"}[name], g)])
                    take(bank, stack_ready, n)
                    biased = name in ("q0", "k0")
                    mm = nc.tensor.matmul(ps[bank][:, 0:width], stack_w(name, j), src, start=True, stop=not biased)
                    if biased:
                        i = 0 if name == "q0" else 1
                        mm = nc.tensor.matmul(ps[bank][:, 0:width], bsl[:, i, j * P:(j + 1) * P], onesr[:, 0:width],
                                              start=False, stop=True)
                    mm.then_inc(stack_mm, 1)
                elif kind == "turn":
                    _, name, g = e
                    src = TURN[name][0]
                    if name[0] == "o":
                        pe.wait_ge(o_ready, nth[("out_norm", int(name[1]), 2 * g + 1)])
                    else:
                        pe.wait_ge(ln_done, nth[("ln_norm", name, g)])
                    take(5, turn_ready, n)
                    for t in range(T):
                        mm = nc.tensor.transpose(ps[5][:, t * P:(t + 1) * P], src[:, g, t, :], ident)
                    mm.then_inc(turn_mm, 1)
                elif kind == "square":
                    _, name, g = e
                    slot = 1 if name[0] == "o" else 0
                    turned = {"v1": "x2", "f": "c"}.get(name, name)
                    pe.wait_ge(turn_ready, nth[("turn", turned, g)])
                    take(4, sq_read, n)
                    for t in range(T):
                        mm = nc.tensor.matmul(ps[4][:, t * P:(t + 1) * P], tT[:, g, slot, t * P:(t + 1) * P],
                                              square_w(name), start=True, stop=True)
                    mm.then_inc(sq_mm, 1)
                elif kind == "max":
                    _, a, b, u = e
                    g, bank = b // 2, n % 2
                    take(bank, max_read, n)
                    o = ps[bank]
                    q0 = (b % 2) * S
                    if a != 1:
                        if u == 0:
                            pe.wait_ge(stack_ready, nth[("stack", f"q{a}", g, QUADS - 1)])
                        qt, half = u // 2, u % 2
                        for i in range(2):
                            j = 2 * half + i
                            mm = nc.tensor.matmul(o[:, i * S:(i + 1) * S], QS[:, g, j, q0 + qt * P:q0 + (qt + 1) * P],
                                                  KBX[:, j, b, :, :].rearrange("p h k -> p (h k)"), start=True, stop=True)
                    else:
                        if u == 0:
                            pe.wait_ge(kb_ready, b + 1)
                            pe.wait_ge(stack_ready, nth[("stack", "q1", g, QUADS - 1)])
                        kb = kbs[b % 2]
                        if u < 4:
                            v = o[:].rearrange("p (h k) -> p h k", h=4)
                            nc.tensor.matmul(v, QS[:, g, u, q0:q0 + P], kb[:, u, :, 0:P], start=True, stop=True)
                            mm = nc.tensor.matmul(v, identr[:], trir[:, 0, :].unsqueeze(1).broadcast_to([P, 4, P]),
                                                  start=False, stop=True, skip_group_check=True)
                        else:
                            j, hh0 = (u - 4) // 2, 2 * ((u - 4) % 2)
                            v = o[:].rearrange("p (h k) -> p h k", h=2)
                            nc.tensor.matmul(v, QS[:, g, j, q0 + P:q0 + 2 * P], kb[:, j, hh0:hh0 + 2, :], start=True, stop=True)
                            mm = nc.tensor.matmul(v[:, :, P:2 * P], identr[:],
                                                  trir[:, 0, :].unsqueeze(1).broadcast_to([P, 2, P]),
                                                  start=False, stop=True, skip_group_check=True)
                    mm.then_inc(max_mm, 1)
                elif kind == "negmax":
                    pe.wait_ge(neg_ready, n)
                    take(5, negT_ready, n)
                    for t in range(2):
                        mm = nc.tensor.transpose(ps[5][:, t * P:(t + 1) * P], MP[:, n % 2, t, :], ident)
                    mm.then_inc(neg_mm, 1)
                elif kind == "scores":
                    _, a, b, u = e
                    g, bank = b // 2, 2 + n % 2
                    k = nth[("negmax", a, b)]
                    if u == 0:
                        pe.wait_ge(negT_ready, k)
                    take(bank, pr_ready, n)
                    o = ps[bank]
                    q0 = (b % 2) * S
                    mt = MT[:, k % 2, :]
                    if a != 1:
                        for i in range(2):
                            p = 2 * u + i
                            nc.tensor.matmul(o[:, i * S:(i + 1) * S],
                                             KBX[:, p // 2, b, 2 * (p % 2):2 * (p % 2) + 2, :].rearrange("p h k -> p (h k)"),
                                             QS[:, g, p // 2, q0:q0 + S], start=True, stop=False)
                            mm = nc.tensor.matmul(o[:, i * S:(i + 1) * S],
                                                  pairsel[:, p, :],
                                                  mt, start=False, stop=True)
                    else:
                        kb = kbs[b % 2]
                        j, h = u // 4, u % 4
                        row_h = identr[:, u:u + 1].broadcast_to([P, P])
                        nc.tensor.matmul(o[:, 0:S], kb[:, j, h, 0:P], QS[:, g, j, q0:q0 + S], start=True, stop=True)
                        nc.tensor.matmul(o[:, S:S + P], kb[:, j, h, P:2 * P], QS[:, g, j, q0 + P:q0 + S], start=False,
                                         stop=True, skip_group_check=True)
                        nc.tensor.matmul(o[:, 0:S], row_h, mt, start=False, stop=True, skip_group_check=True)
                        nc.tensor.matmul(o[:, S:S + P], row_h, mt[:, P:S], start=False, stop=True, skip_group_check=True)
                        for c in (0, S):
                            mm = nc.tensor.matmul(o[:, c:c + P], identr[:], trir[:, 1, :], start=False, stop=True,
                                                  skip_group_check=True)
                    mm.then_inc(sc_mm, 1)
                elif kind == "pv":
                    _, a, b, u = e
                    g = b // 2
                    pe.wait_ge(pr_ready, n)
                    if u == 0:
                        take(4, o_ready, nth[("out_norm", a, b)])
                        if a == 1:
                            pe.wait_ge(sq_read, nth[("square", "v1", g)])
                    prob = pr[:, n % 4, :]
                    if a != 1:
                        for i in range(2):
                            p = 2 * u + i
                            for qt in range(2):
                                c = qt * H * DV + p * 2 * DV
                                mm = nc.tensor.matmul(ps[4][:, c:c + 2 * DV], prob[:, i * S + qt * P:i * S + (qt + 1) * P],
                                                      VBX[:, a // 2, b, p, :], start=True, stop=True)
                    else:
                        t0 = 2 * (b % 2)
                        c = u * DV
                        nc.tensor.matmul(ps[4][:, c:c + DV], prob[:, 0:P], VS[:, g, t0, u, :], start=True, stop=True)
                        c += H * DV
                        nc.tensor.matmul(ps[4][:, c:c + DV], prob[:, P:2 * P], VS[:, g, t0, u, :], start=True, stop=False)
                        mm = nc.tensor.matmul(ps[4][:, c:c + DV], prob[:, S:S + P], VS[:, g, t0 + 1, u, :],
                                              start=False, stop=True)
                    mm.then_inc(pv_done, 1)
                elif kind == "gate0":
                    g = e[1]
                    pe.wait_ge(turn_ready, nth[("turn", "x1", g)])
                    take(4, g0_lg, n)
                    for t in range(T):
                        mm = nc.tensor.matmul(ps[4][:, t * 8:(t + 1) * 8], tT[:, g, 0, t * P:(t + 1) * P], wg[:, 0, :],
                                              start=True, stop=True)
                    mm.then_inc(g0_mm, 1)
                elif kind == "up0":
                    _, g, x_ = e
                    if n == 1:
                        pe.wait_ge(in_w0, 16)
                    pe.wait_ge(turn_ready, nth[("turn", "x1", g)])
                    bank = n % 4
                    take(bank, relu_ready, n)
                    nc.tensor.matmul(ps[bank][:], we0[:, 0, x_ * P:(x_ + 1) * P], tT[:, g, 0, :], start=True,
                                     stop=True).then_inc(up0_mm, 1)
                elif kind == "down0":
                    _, g, x_ = e
                    pe.wait_ge(h0_ready, n)
                    bank = 6 + n % 2
                    take(bank, dn0_read, n)
                    for t in range(T):
                        mm = nc.tensor.matmul(ps[bank][:, t * P:(t + 1) * P], hh[:, n % 3, t * P:(t + 1) * P],
                                              we0[:, 1, x_ * P:(x_ + 1) * P], start=True, stop=True)
                    mm.then_inc(dn0_mm, 1)
                elif kind == "gate1":
                    g = e[1]
                    take(4, g1_sub, n)
                    for t in range(T):
                        mm = nc.tensor.matmul(ps[4][:, t * 8:(t + 1) * 8], tT[:, g, 0, t * P:(t + 1) * P], wg[:, 1, :],
                                              start=True, stop=True)
                    mm.then_inc(g1_mm, 1)
                elif kind == "up1":
                    _, x_, g, c = e
                    pe.wait_ge(w_ready, x_ + 1)
                    pe.wait_ge(xs_ready, g + 1)
                    pair = 2 * (n % 2)
                    take(pair, h1_ready, n)
                    take(pair + 1, silu_ready, n)
                    for part in range(2):
                        hi, lo = hi_lo(x_, part, c)
                        o = ps[pair + part][:]
                        nc.tensor.matmul(o, hi, XH[:, g, :], start=True, stop=False)
                        nc.tensor.matmul(o, hi, XL[:, g, :], start=False, stop=False)
                        mm = nc.tensor.matmul(o, lo, XH[:, g, :], start=False, stop=True)
                    mm.then_inc(up1_mm, 1)
                elif kind == "down1":
                    _, x_, g, c = e
                    pe.wait_ge(lo_ready, n)
                    bank = 6 + g
                    if c == 0:
                        take(bank, dn1_read, nth[("add1", x_, g)])
                    hi, lo = hi_lo(x_, 2, c)
                    for t in range(T):
                        o = ps[bank][:, t * P:(t + 1) * P]
                        ah, al = hhi[:, n % 3, t * P:(t + 1) * P], hlo[:, n % 3, t * P:(t + 1) * P]
                        nc.tensor.matmul(o, ah, hi, start=(c == 0 and t == 0), stop=False, skip_group_check=True)
                        nc.tensor.matmul(o, ah, lo, start=False, stop=False, skip_group_check=True)
                        mm = nc.tensor.matmul(o, al, hi, start=False, stop=(c == CH - 1), skip_group_check=True)
                    if c == CH - 1:
                        mm.then_inc(dn1_mm, 1)
                    else:
                        mm.then_inc(dn1_chunk, 1)

        @block.scalar
        def _(sc):
            for e in ev:
                kind, n = e[0], nth[e]
                if kind == "ctx":
                    sc.wait_ge(ctx_turned, 1)
                    nc.scalar.copy(cxT[:], ps[5][:, 0:B * SC]).then_inc(ctx_ready, 1)
                    nc.scalar.copy(cxT2[:], ps[5][:, 0:B * SC].rearrange("p (b k) -> p b k", b=B).unsqueeze(2)
                                   .broadcast_to([P, B, 2, SC])).then_inc(ctx_ready, 1)
                elif kind == "stack":
                    _, name, g, j = e
                    width = B * SC if name in ("k0", "k2") else GT
                    sc.wait_ge(stack_mm, n)
                    if n > 2:
                        sc.wait_ge(stack_ready, n - 2)
                    nc.scalar.activation(T1[:, n % 2, 0:width], ps[6 + n % 2][:, 0:width], ACT.Copy,
                                         scale=sign[name[0] + "b"]).then_inc(stack_high, 1)
                elif kind == "turn":
                    _, name, g = e
                    sc.wait_ge(turn_mm, n)
                    nc.scalar.copy(tT[:, g, TURN[name][1], :], ps[5][:]).then_inc(turn_ready, 1)
                elif kind == "negmax":
                    sc.wait_ge(neg_mm, n)
                    nc.scalar.copy(MT[:, n % 2, :], ps[5][:, 0:S]).then_inc(negT_ready, 1)
                elif kind == "scores":
                    _, a, b, u = e
                    sc.wait_ge(sc_mm, n)
                    if n > 4:
                        sc.wait_ge(pv_done, n - 4)
                    width = GT if a != 1 else S + P
                    nc.scalar.activation(pr[:, n % 4, 0:width], ps[2 + n % 2][:, 0:width], ACT.Exp,
                                         scale=SCALE[a]).then_inc(pr_ready, 1)
                elif kind == "gate0":
                    sc.wait_ge(g0_lg, n)
                    nc.scalar.activation(ex[:], lg[:], ACT.Exp, scale=-1.0).then_inc(g0_exp, 1)
                elif kind == "up0":
                    sc.wait_ge(up0_mm, n)
                    if n > 3:
                        sc.wait_ge(h0_ready, n - 3)
                    nc.scalar.activation(hr[:, n % 3, :], ps[n % 4][:], ACT.Relu).then_inc(relu_ready, 1)
                elif kind == "gate1":
                    sc.wait_ge(g1_sub, n)
                    nc.scalar.activation(ex[:], zz[:], ACT.Exp).then_inc(g1_exp, 1)
                elif kind == "up1":
                    sc.wait_ge(up1_mm, n)
                    if n > 3:
                        sc.wait_ge(h1_ready, n - 3)
                    nc.scalar.activation(hr[:, n % 3, :], ps[2 * (n % 2) + 1][:], ACT.Silu).then_inc(silu_ready, 1)
                    sc.wait_ge(h1_ready, n)
                    if n > 3:
                        sc.wait_ge(dn1_chunk, (n - 3) - (n - 3) // CH)
                        if (n - 3) // CH:
                            sc.wait_ge(dn1_mm, (n - 3) // CH)
                    nc.scalar.copy(hhi[:, n % 3, :], hh[:, n % 3, :]).then_inc(hi_ready, 1)

        @block.vector
        def _(dve):
            step = [0]

            def link(ins):
                step[0] += 1
                ins.then_inc(dve_step, 1)
                dve.wait_ge(dve_step, step[0])

            dve.wait_ge(in_cst, 16)
            nc.vector.tensor_copy(identr[:], ident).then_inc(const_ready, 1)
            nc.vector.tensor_copy(trir[:].rearrange("p a k -> p (a k)"),
                                  cst[:, CONST["tri_q"]:CONST["tri_q"] + 2 * P]).then_inc(const_ready, 1)
            nc.vector.tensor_copy(pairsel[:].rearrange("p a (h k) -> p (a h) k", h=2),
                                  cst[:, 0:H].unsqueeze(2).broadcast_to([P, H, SC])).then_inc(const_ready, 1)
            nc.vector.memset(onesr[:].bitcast(F32), 1.0).then_inc(const_ready, 1)
            for e in ev:
                kind, n = e[0], nth[e]
                if kind == "bias":
                    dve.wait_ge(bias_rows, 32)
                    link(nc.vector.tensor_scalar(bhi[:], braw[:], sign["bb"], None, ALU.mult))
                    dve.wait_ge(const_ready, 4)
                    nc.vector.scalar_tensor_tensor(bsl[:], braw[:], sign["ba"], bhi[:].bitcast(F32), ALU.mult,
                                                   ALU.add).then_inc(bias_ready, 1)
                elif kind == "vctx":
                    dve.wait_ge(vctx_mm, n)
                    dve.wait_ge(zeroed, 9)
                    dve.wait_ge(in_small, 48)
                    for half in range(2):
                        pp = slice(64 * half, 64 * half + 64)
                        src = ps[4][pp, :].rearrange("p (b e two d) -> p b e two d", b=B, two=2, d=D)
                        dst = VBX[pp, e[1] // 2, :, :, :].rearrange("p b e (two d) -> p b e two d", two=2)
                        for b in range(B):
                            o, i = dst[:, b, :, half, 0:D], src[:, b, :, half, :]
                            if e[1] == 0:
                                bias = row("bv")[pp, :].rearrange("p (e two d) -> p e two d", two=2, d=D)[:, :, half, :]
                                ins = nc.vector.tensor_tensor(o, i, bias, ALU.add)
                            else:
                                ins = nc.vector.tensor_copy(o, i)
                    ins.then_inc(vctx_ready, 1)
                elif kind == "stack":
                    _, name, g, j = e
                    width = B * SC if name in ("k0", "k2") else GT
                    dve.wait_ge(stack_high, n)
                    src, t1 = ps[6 + n % 2], T1[:, n % 2, :].bitcast(F32)
                    sa = sign[name[0] + "a"]
                    if name in ("k0", "k2"):
                        if n == 1:
                            dve.wait_ge(zeroed, 9)
                        for h in range(4):
                            pp = slice(SLOT * h, SLOT * (h + 1))
                            ins = nc.vector.scalar_tensor_tensor(
                                KBX[pp, j, :, h, :], src[pp, 0:width].rearrange("p (b k) -> p b k", b=B), sa[pp, :],
                                t1[pp, 0:width].rearrange("p (b k) -> p b k", b=B), ALU.mult, ALU.add)
                    else:
                        dst = QS[:, g, j, :] if name[0] == "q" else KS[:, j, :]
                        ins = nc.vector.scalar_tensor_tensor(dst, src[:], sa, t1, ALU.mult, ALU.add)
                    ins.then_inc(stack_ready, 1)
                elif kind == "kblocks":
                    b = e[2]
                    dve.wait_ge(stack_ready, nth[("stack", "k1", b // 2, QUADS - 1)])
                    if b >= 2:
                        dve.wait_ge(sc_mm, nth[("scores", 1, b - 2, 15)])
                    for h in range(4):
                        pp = slice(SLOT * h, SLOT * (h + 1))
                        ins = nc.vector.tensor_copy(kbs[b % 2][pp, :, h, :],
                                                    KS[pp, :, (b % 2) * S:(b % 2) * S + S].bitcast(F32))
                    ins.then_inc(kb_ready, 1)
                elif kind == "ln_stats":
                    _, name, g = e
                    src = LN[name][0]
                    if name == "x0" and g == 0:
                        dve.wait_ge(in_x, 16)
                    for t in range(T):
                        ins = nc.vector.bn_stats(stat[:, t, :], src[:, g, t, :])
                    link(ins)
                    for t in range(T):
                        ins = nc.vector.bn_aggr(mv[:, n - 1, t, :], stat[:, t, :])
                    ins.then_inc(ln_stat, 1)
                elif kind == "ln_norm":
                    _, name, g = e
                    src, dst, _, affine = LN[name]
                    k = nth[("ln_stats", name, g)] - 1
                    dve.wait_ge(ln_rstd, k + 1)
                    for t in range(T):
                        ins = nc.vector.tensor_scalar(dst[:, g, t, :], src[:, g, t, :], mv[:, k, t, 0:1], rstd[:, k, t:t + 1],
                                                      ALU.subtract, ALU.mult)
                    if affine:
                        link(ins)
                        link(nc.vector.tensor_tensor(dst[:, g], dst[:, g], rows4(affine[0]), ALU.mult))
                        ins = nc.vector.tensor_tensor(dst[:, g], dst[:, g], rows4(affine[1]), ALU.add)
                    if name == "f":
                        link(ins)
                        ins = nc.vector.tensor_tensor(X[:, g], X[:, g], act[:, g], ALU.add)
                    ins.then_inc(ln_done, 1)
                    dve.wait_ge(ln_done, n)
                elif kind == "max":
                    _, a, b, u = e
                    dve.wait_ge(max_mm, n)
                    k = nth[("negmax", a, b)]
                    src = ps[n % 2][:]
                    if a != 1:
                        o, heads = MX[:, k % 2, u // 2, 8 * (u % 2):8 * (u % 2) + 8], 8
                    elif u < 4:
                        o, heads = MX[:, k % 2, 0, 4 * u:4 * u + 4], 4
                    else:
                        o, heads = MX[:, k % 2, 1, 2 * (u - 4):2 * (u - 4) + 2], 2
                    nc.vector.tensor_reduce(o, src.rearrange("p (h k) -> p h k", h=heads), AX_X, ALU.max).then_inc(max_read, 1)
                elif kind == "negmax":
                    _, a, b = e
                    dve.wait_ge(max_read, nth[("max", a, b, 11 if a == 1 else 3)])
                    if n == 1:
                        dve.wait_ge(zeroed, 9)
                    if n > 2:
                        dve.wait_ge(neg_mm, n - 2)
                    nc.vector.tensor_scalar(MP[:, n % 2, :, 0:H], MX[:, n % 2], -1.0, None, ALU.mult).then_inc(neg_ready, 1)
                elif kind == "out_norm":
                    _, a, b = e
                    dve.wait_ge(pv_done, nth[("pv", a, b, 15 if a == 1 else 3)])
                    v = ps[4][:, 0:2 * H * DV].rearrange("p (q h d) -> p q h d", q=2, d=DV)
                    link(nc.vector.reciprocal(rec[:], v[:, :, :, D]))
                    if b % 2 == 0 and a > 0:
                        dve.wait_ge(turn_mm, nth[("turn", f"o{a - 1}", b // 2)])
                    for q in range(2):
                        ins = nc.vector.tensor_tensor(
                            o_n[:, b // 2, 2 * (b % 2) + q, :].rearrange("p (h d) -> p h d", d=D), v[:, q, :, 0:D],
                            rec[:, q, :].unsqueeze(2).broadcast_to([P, H, D]), ALU.mult)
                    ins.then_inc(o_ready, 1)
                elif kind == "square":
                    _, name, g = e
                    dve.wait_ge(sq_mm, n)
                    y = ps[4][:].rearrange("p (t d) -> p t d", t=T)
                    if name == "o0":
                        dve.wait_ge(xb_ready, g + 1)
                        ins = nc.vector.tensor_tensor(X[:, g], y, xb[:, g], ALU.add)
                    elif name == "v1":
                        if g == 0:
                            dve.wait_ge(zeroed, 9)
                        for t in range(T):
                            ins = nc.vector.tensor_copy(VS[:, g, t, :, 0:D], y[:, t, :].rearrange("p (h d) -> p h d", d=D))
                    elif name == "o1":
                        link(nc.vector.tensor_tensor(act[:, g], y, rows4("bo1"), ALU.add))
                        ins = nc.vector.scalar_tensor_tensor(act[:, g], act[:, g], 0.0, lni[:, g], ALU.max, ALU.add)
                    elif name == "o2":
                        link(nc.vector.tensor_tensor(act[:, g], y, rows4("bo2"), ALU.add))
                        ins = nc.vector.tensor_scalar(act[:, g], act[:, g], 0.0, 2.0, ALU.max, ALU.mult)
                    else:
                        link(nc.vector.tensor_tensor(act[:, g], y, rows4("bf"), ALU.add))
                        ins = nc.vector.scalar_tensor_tensor(act[:, g], act[:, g], 0.0, lnx[:, g], ALU.max, ALU.add)
                    ins.then_inc(sq_read, 1)
                    dve.wait_ge(sq_read, n)
                elif kind == "gate0":
                    g = e[1]
                    dve.wait_ge(g0_mm, n)
                    nc.vector.tensor_copy(lg[:].rearrange("p t x -> p (t x)"), ps[4][:, 0:8 * T]).then_inc(g0_lg, 1)
                    dve.wait_ge(g0_lg, n)
                    lb = rowb[:, len(ROWS) * P:len(ROWS) * P + 8]
                    link(nc.vector.tensor_tensor(zz[:], lg[:], lb.unsqueeze(1).broadcast_to([P, T, 8]), ALU.add))
                    for t in range(T):
                        ins = nc.vector.max(m8[:, t, :], zz[:, t, :])
                    link(ins)
                    for t in range(T):
                        ins = nc.vector.max_index(i8[:, t, :], m8[:, t, :], zz[:, t, :])
                    link(ins)
                    link(nc.vector.tensor_copy(i8f[:], i8[:]))
                    for k in range(2):
                        ins = nc.vector.tensor_tensor(sel[:, k], iota.unsqueeze(1).broadcast_to([P, T, 8]),
                                                      i8f[:, :, k:k + 1].broadcast_to([P, T, 8]), ALU.is_equal)
                    link(ins)
                    link(nc.vector.tensor_tensor(sel[:, 0], sel[:, 0], sel[:, 1], ALU.add))
                    dve.wait_ge(g0_exp, n)
                    link(nc.vector.tensor_scalar(zz[:], ex[:], 1.0, None, ALU.add))
                    link(nc.vector.reciprocal(zz[:], zz[:]))
                    link(nc.vector.tensor_tensor(zz[:], zz[:], sel[:, 0], ALU.mult))
                    link(nc.vector.tensor_reduce(r1[:], zz[:], AX_X, ALU.add))
                    link(nc.vector.tensor_scalar(r1[:], r1[:], 1e-6, None, ALU.add))
                    link(nc.vector.reciprocal(r2[:], r1[:]))
                    nc.vector.tensor_tensor(wt[:, 0, g], zz[:], r2[:].broadcast_to([P, T, 8]), ALU.mult).then_inc(g0_ready, 1)
                    dve.wait_ge(g0_ready, n)
                elif kind == "up0":
                    dve.wait_ge(relu_ready, n)
                    if n > 3:
                        dve.wait_ge(dn0_mm, n - 3)
                    nc.vector.tensor_tensor(hh[:, n % 3, :], hr[:, n % 3, :], hr[:, n % 3, :], ALU.mult).then_inc(h0_ready, 1)
                elif kind == "down0":
                    _, g, x_ = e
                    dve.wait_ge(dn0_mm, n)
                    if x_ > 0:
                        dve.wait_ge(dn0_read, n - 1)
                    y = ps[6 + n % 2][:].rearrange("p (t d) -> p t d", t=T)
                    if x_ == E0 - 1:
                        ins = nc.vector.tensor_tensor(X[:, g], y, X[:, g], ALU.add)
                    else:
                        for t in range(T):
                            ins = nc.vector.scalar_tensor_tensor(X[:, g, t, :], y[:, t, :], wt[:, 0, g, t, x_:x_ + 1],
                                                                 X[:, g, t, :], ALU.mult, ALU.add)
                    ins.then_inc(dn0_read, 1)
                    if x_ == E0 - 1:
                        dve.wait_ge(dn0_read, n)
                elif kind == "xsplit":
                    g = e[1]
                    dve.wait_ge(turn_ready, nth[("turn", "x3", g)])
                    link(nc.vector.tensor_copy(XH[:, g, :], tT[:, g, 0, :]))
                    nc.vector.tensor_tensor(XL[:, g, :], tT[:, g, 0, :], XH[:, g, :].bitcast(F32),
                                            ALU.subtract).then_inc(xs_ready, 1)
                elif kind == "gate1":
                    g = e[1]
                    dve.wait_ge(g1_mm, n)
                    link(nc.vector.tensor_copy(lg[:].rearrange("p t x -> p (t x)"), ps[4][:, 0:8 * T]))
                    link(nc.vector.tensor_reduce(r1[:], lg[:], AX_X, ALU.max))
                    nc.vector.tensor_tensor(zz[:], lg[:], r1[:].broadcast_to([P, T, 8]), ALU.subtract).then_inc(g1_sub, 1)
                    dve.wait_ge(g1_exp, n)
                    link(nc.vector.tensor_reduce(r1[:], ex[:], AX_X, ALU.add))
                    link(nc.vector.reciprocal(r2[:], r1[:]))
                    link(nc.vector.tensor_tensor(zz[:], ex[:], r2[:].broadcast_to([P, T, 8]), ALU.mult))
                    for t in range(T):
                        ins = nc.vector.max(m8[:, t, :], zz[:, t, :])
                    link(ins)
                    for t in range(T):
                        ins = nc.vector.max_index(i8[:, t, :], m8[:, t, :], zz[:, t, :])
                    link(ins)
                    link(nc.vector.tensor_copy(i8f[:], i8[:]))
                    link(nc.vector.tensor_tensor(sel[:, 0], iota.unsqueeze(1).broadcast_to([P, T, 8]),
                                                 i8f[:, :, 0:1].broadcast_to([P, T, 8]), ALU.is_equal))
                    link(nc.vector.tensor_tensor(sel[:, 0], sel[:, 0], m8[:, :, 0:1].broadcast_to([P, T, 8]), ALU.mult))
                    nc.vector.tensor_scalar(wt[:, 1, g], sel[:, 0], 2.0, None, ALU.mult).then_inc(g1_ready, 1)
                    dve.wait_ge(g1_ready, n)
                elif kind == "up1":
                    dve.wait_ge(silu_ready, n)
                    if n > 3:
                        dve.wait_ge(hi_ready, n - 3)
                    nc.vector.tensor_tensor(hh[:, n % 3, :], ps[2 * (n % 2)][:], hr[:, n % 3, :], ALU.mult).then_inc(h1_ready, 1)
                    dve.wait_ge(hi_ready, n)
                    if n > 3:
                        dve.wait_ge(dn1_chunk, (n - 3) - (n - 3) // CH)
                        if (n - 3) // CH:
                            dve.wait_ge(dn1_mm, (n - 3) // CH)
                    nc.vector.tensor_tensor(hlo[:, n % 3, :], hh[:, n % 3, :], hhi[:, n % 3, :].bitcast(F32),
                                            ALU.subtract).then_inc(lo_ready, 1)
                elif kind == "add1":
                    _, x_, g = e
                    dve.wait_ge(dn1_mm, n)
                    if n > 2:
                        dve.wait_ge(dn1_read, n - 2)
                    y = ps[6 + g][:].rearrange("p (t d) -> p t d", t=T)
                    if x_ == 0:
                        ins = nc.vector.tensor_tensor(X[:, g], y, X[:, g], ALU.add)
                    else:
                        for t in range(T):
                            k = order(x_)
                            ins = nc.vector.scalar_tensor_tensor(X[:, g, t, :], y[:, t, :], wt[:, 1, g, t, k:k + 1],
                                                                 X[:, g, t, :], ALU.mult, ALU.add)
                    ins.then_inc(dn1_read, 1)


def _pack(inputs):
    f = {k: np.ascontiguousarray(v) for k, v in inputs.items()}

    def stack(w):
        w = w.reshape(w.shape[0], QUADS, 4, 1, D)
        w = np.concatenate([w, w, w, np.zeros_like(w)], axis=3)
        return w.reshape(w.shape[0], QUADS * P)

    def per_head(w):
        return w.transpose(1, 0, 2).reshape(P, P)

    const = np.zeros((P, NCONST), np.float32)
    const[:, 0:P] = np.eye(P)
    q, k = np.meshgrid(np.arange(P), np.arange(P), indexing="ij")
    const[:, P:2 * P] = np.where(k > q, NEG, 0.0)
    const[:, 2 * P:3 * P] = np.where(q > k, NEG, 0.0)
    third = (np.arange(P) % SLOT) // D
    for i, low in ((0, 2), (2, 1)):
        const[:, 384 + i] = third == low
        const[:, 385 + i] = np.where(third == low, -1.0, 1.0)
    const[:, 388] = np.arange(P) == 1
    const[:, 389] = np.where(np.arange(P) == 1, -1.0, 1.0)
    const[:, 390:398] = np.arange(8)
    stacks = np.stack([stack(w) for w in (
        f["L0_xattn_Wk"].T, f["L0_xattn_Wq"].T, per_head(f["L1_xattn_Wk1"]), per_head(f["L1_xattn_Wq1"]),
        per_head(f["L1_xattn_Wk2"]), per_head(f["L1_xattn_Wq2"]))], axis=1)
    squares = np.stack([f["L0_xattn_Wv"].T, f["L0_xattn_Wo"].T, per_head(f["L1_xattn_Wv1"]), f["L1_xattn_Wo1"],
                        per_head(f["L1_xattn_Wv2"]), f["L1_xattn_Wo2"], f["L1_xattn_Wf"]], axis=1)
    rows = np.concatenate([f[n] for n in (
        "L0_xattn_bv", "L0_xattn_bo", "L1_xattn_bo1", "L1_xattn_g1", "L1_xattn_b1", "L1_xattn_bo2", "L1_xattn_g2",
        "L1_xattn_b2", "L1_xattn_bf", "L1_xattn_g3", "L1_xattn_b3", "L0_ffn_lb_bias")])
    w0 = np.stack([
        np.concatenate([f["L0_ffn_w1"].transpose(2, 0, 1).reshape(P, -1), f["L0_ffn_cfc"].T], axis=1),
        np.concatenate([f["L0_ffn_w2"].transpose(2, 0, 1).reshape(P, -1), f["L0_ffn_cproj"].T], axis=1)], axis=1)

    def down(w):
        return w.reshape(-1, CH, P, P).transpose(2, 0, 1, 3).reshape(P, -1, HID)

    w1 = np.concatenate([
        np.concatenate([f["L1_ffn_w_up"], f["L1_ffn_ws_up"][None]]).transpose(1, 0, 2),
        np.concatenate([f["L1_ffn_w_gate"], f["L1_ffn_ws_gate"][None]]).transpose(1, 0, 2),
        down(np.concatenate([f["L1_ffn_w_down"], f["L1_ffn_ws_down"][None]]))], axis=2)
    return {
        "x": f["x"].reshape(-1, P), "ctx": f["ctx_1024"].reshape(-1, P), "const": const, "stacks": stacks,
        "qkbias": np.stack([stack(f["L0_xattn_bq"][None])[0], stack(f["L0_xattn_bk"][None])[0]])[None],
        "squares": squares, "rows": rows,
        "gates": np.stack([f["L0_ffn_gate_w"].T, f["L1_ffn_w_router"]], axis=1), "w0": w0, "w1": w1,
    }


def kernel(**inputs):
    import concourse.bacc as _bacc
    from concourse.bass_utils import run_bass_kernel_spmd as _run

    nc = _bacc.Bacc("TRN2", target_bir_lowering=False, num_devices=1)
    arrays, args = {}, []
    for name, a in _pack({k: np.asarray(v) for k, v in inputs.items()}).items():
        a = np.ascontiguousarray(a)
        arrays[f"in_{name}"] = a
        args.append(nc.dram_tensor(f"in_{name}", a.shape, mybir.dt.from_np(a.dtype), kind="ExternalInput").ap())
    out = nc.dram_tensor("out", (B * S, P), F32, kind="ExternalOutput").ap()
    build(nc, *args, out)
    r = _run(nc, [arrays], core_ids=[0])
    return r.results[0]["out"].reshape(B, S, P)
```

```python
from contextlib import ExitStack

import numpy as np
import concourse.bass as bass
import concourse.mybir as mybir

ALU = mybir.AluOpType
ACT = mybir.ActivationFunctionType
F32 = mybir.dt.float32
F16 = mybir.dt.float16
BF16 = mybir.dt.bfloat16
U32 = mybir.dt.uint32
AX_X = mybir.AxisListType.X

P = 128
B, S, SC = 4, 256, 64
H, D = 16, 8
G, T = 2, 4
GT = T * P
QUADS, SLOT = 4, 32
E0 = 9
E1, HID, CH = 8, 512, 4
NEG = -1.0e30
DV = D + 1
NPV = 3

ROWS = ["bv", "bo", "bo1", "g1", "b1", "bo2", "g2", "b2", "bf", "g3", "b3"]
CONST = {"ident": 0, "tri_q": 128, "tri_k": 256, "signs": 384, "iota": 390, "heads": 398}
NCONST = 414
PIECE = 3 * HID
WEIGHTS = {}
for _a, _piece in enumerate((0, 3, 4)):
    WEIGHTS[f"k{_a}"] = (_piece, 0)
    WEIGHTS[f"q{_a}"] = (_piece, QUADS * P)
    WEIGHTS[f"v{_a}"] = (_piece, 2 * QUADS * P)
    WEIGHTS[f"o{_a}"] = (_piece, 2 * QUADS * P + P)
WEIGHTS["f"] = (4, 2 * QUADS * P + 2 * P)
WEIGHTS["up0"], WEIGHTS["down0"] = (1, 0), (2, 0)
FIRST1 = 5
PIECES = FIRST1 + E1
USED = [1280, 1152, 1152, 1280, 1408] + [PIECE] * E1

COST = {"max": 0.45, "scores": 0.7, "pv": 0.3, "stack": 0.8, "turn": 1.5, "square": 1.6, "ln_stats": 1.5,
        "ln_norm": 2.0, "up": 1.3, "down": 0.7, "gate0": 4.0, "gate1": 4.0, "kblocks": 1.3, "negmax": 1.0,
        "out_norm": 0.8, "add1": 0.6, "plow": 0.1, "hi": 0.1}


def attention(a, g):
    nmax, nst = (12, 16) if a == 1 else (4, 4)

    def maxima(b):
        return [("max", a, b, u) for u in range(nmax)] + [("negmax", a, b)]

    def values(b):
        out = []
        for u in range(nst + 2):
            out += [("scores", a, b, u)] if u < nst else []
            out += [("plow", a, b, u - 1)] if 1 <= u <= nst else []
            out += [("pv", a, b, u - 2)] if u >= 2 else []
        return out + [("out_norm", a, b)]

    b = 2 * g
    out = [("kblocks", a, b)] if a == 1 else []
    out += maxima(b)
    nxt = ([("kblocks", a, b + 1)] if a == 1 else []) + maxima(b + 1)
    steps = values(b)
    out += weave(steps[:-6], nxt, 0.0) + steps[-6:] + values(b + 1)
    return out + [("turn", f"o{a}", g), ("square", f"o{a}", g)]


def weave(a, b, lag, after=None):
    out, placed, i, j, ta, tb = [], set(), 0, 0, 0.0, lag
    while i < len(a) or j < len(b):
        blocked = j < len(b) and after and after.get(b[j]) not in (None, *placed)
        if i < len(a) and (j == len(b) or ta <= tb or blocked):
            out.append(a[i])
            ta += COST.get(a[i][0], 0.5)
            i += 1
            if blocked:
                tb = max(tb, ta)
        else:
            out.append(b[j])
            tb += COST.get(b[j][0], 0.5)
            j += 1
        placed.add(out[-1])
    return out


def stream(g):
    def normed(name):
        return [("ln_stats", name, g), ("ln_norm", name, g), ("turn", name, g)]

    def stack(name):
        return [("stack", name, g, j) for j in range(QUADS)]

    ev = normed("x0") + stack("q0") + attention(0, g)
    ev += normed("x1") + [("gate0", g)]
    for e in range(E0 + 2):
        ev += [("up", 0, g, e, 0)] if e < E0 else []
        ev += [("hi", 0, g, e - 1, 0)] if 1 <= e <= E0 else []
        ev += [("down", 0, g, e - 2, 0)] if e >= 2 else []
    ev += normed("x2") + stack("k1") + stack("q1") + [("square", "v1", g)] + attention(1, g)
    ev += normed("a") + stack("q2") + attention(2, g)
    ev += normed("c") + [("square", "f", g)]
    ev += [("ln_stats", "f", g), ("ln_norm", "f", g)] + normed("x3")
    steps = [(n, c) for n in range(E1) for c in range(CH)]
    for i in range(len(steps) + 2):
        ev += [("up", 1, g) + steps[i]] if i < len(steps) else []
        ev += [("hi", 1, g) + steps[i - 1]] if 1 <= i <= len(steps) else []
        if i == 1:
            ev += [("gate1", g)]
        if i >= 2:
            n, c = steps[i - 2]
            ev += [("down", 1, g, n, c)]
            ev += [("add1", n, g)] if c == CH - 1 else []
    return ev + [("store", g)]


def schedule():
    ev = [("split", 0), ("ctx",), ("bias",)] + [("stack", "k0", 0, j) for j in range(QUADS)] + [("vctx", 0)]
    after = {("kblocks", 1, 2): ("scores", 1, 0, 15), ("kblocks", 1, 3): ("scores", 1, 1, 15)}
    main = weave(stream(0), stream(1), LAG, after)
    at = max(i for i, e in enumerate(main) if e[:2] in (("max", 0), ("scores", 0)))
    pieces = [("split", i) for i in range(1, PIECES)]
    out = []
    for i, e in enumerate(main):
        out.append(e)
        if i == at:
            out += [("stack", "k2", 0, j) for j in range(QUADS)] + [("vctx", 2)]
        if i > 24 and i % 12 == 0 and pieces:
            out.append(pieces.pop(0))
    assert not pieces
    need = {}
    for i, e in enumerate(out):
        if e[0] == "split":
            need[e[1]] = i
    for i, e in enumerate(out):
        for p in uses(e):
            assert need[p] < i
    return ev + out


LAG = 30.0


def uses(e):
    if e[0] in ("stack", "square") and WEIGHTS[e[1]][0] > 0:
        return [WEIGHTS[e[1]][0]]
    if e[0] == "vctx" and e[1] == 2:
        return [4]
    if e[0] == "up":
        return [1, 2] if e[1] == 0 else [FIRST1 + e[3]]
    return []


def order(n):
    return (E1 - 1 + n) % E1


def build(nc, x, ctx, const, weights, qkbias, rows, gates, out):
    ev = schedule()
    nth, seen = {}, {}
    bank, ring, misc = {}, 0, 0
    for e in ev:
        seen[e[0]] = seen.get(e[0], 0) + 1
        nth[e] = seen[e[0]]
        if e[0] in ("max", "scores", "up"):
            if e[0] == "up" and e[1] == 1:
                ring += ring % 2
                bank[e] = ring % 4
                ring += 2
            else:
                bank[e] = ring % 4
                ring += 1
        elif e[0] == "pv" or (e[0] == "down" and e[1] == 1):
            bank[e] = 4 + (e[2] // 2 if e[0] == "pv" else e[2])
        elif e[0] in ("ctx", "vctx", "stack", "turn", "square", "negmax", "gate0", "gate1", "down"):
            bank[e] = 6 + misc % 2
            misc += 1
    nth_plow_before, nth_hi_before, nth_up_before, buffer = {}, {}, {}, {}
    for g in range(G):
        scores = [e for e in ev if e[0] == "scores" and e[2] // 2 == g]
        ups = [e for e in ev if e[0] == "up" and e[2] == g]
        for i, e in enumerate(scores):
            buffer[e] = i % 2
            if i >= 2:
                nth_plow_before[e] = nth[("plow",) + scores[i - 2][1:]]
        for i, e in enumerate(ups):
            buffer[e] = i % 2
            if i >= 2:
                nth_hi_before[e] = nth[("hi",) + ups[i - 2][1:]]
                nth_up_before[e] = nth[ups[i - 2]]
    nth_down0 = {e: i + 1 for i, e in enumerate(e for e in ev if e[0] == "down" and e[1] == 0)}
    nth_pv_before, last = {}, {}
    for e in ev:
        if e[0] == "scores":
            nth_pv_before[e] = last.get(e[2] // 2, 0)
        elif e[0] == "pv":
            last[e[2] // 2] = nth[e]
    splits = {e[1]: nth[e] for e in ev if e[0] == "split"}
    assert all(splits[i] == i + 1 for i in range(PIECES))

    with ExitStack() as stk:
        def sb(name, shape, dt=F32):
            return stk.enter_context(nc.sbuf_tensor(name, shape, dt))

        def sem(name):
            return stk.enter_context(nc.semaphore(name))

        cst = sb("cst", [P, NCONST])
        identb = sb("identb", [P, P], BF16)
        trib = sb("trib", [P, 2, P], BF16)
        headsel = sb("headsel", [P, H, P], BF16)
        pairsel = sb("pairsel", [P, H, SC], BF16)
        neghalf = sb("neghalf", [P, T])
        rowb = sb("rowb", [P, len(ROWS) * P + 8])
        wg = sb("wg", [P, 2, 8])
        wraw = sb("wraw", [P, 2, PIECE])
        wh = sb("wh", [P, sum(USED)], F16)
        wl = sb("wl", [P, sum(USED)], F16)
        X = sb("X", [P, G, T, P])
        cxs = [sb("cxh", [P, B * SC], F16), sb("cxl", [P, B * SC], F16)]
        cxt = [sb("cxth", [P, B, 2, SC], F16), sb("cxtl", [P, B, 2, SC], F16)]
        stat = sb("stat", [P, T, 6])
        mv = sb("mv", [P, 7 * G, T, 2])
        rstd = sb("rstd", [P, 7 * G, T])
        lnx = sb("lnx", [P, G, T, P])
        lni = sb("lni", [P, G, T, P])
        act = sb("act", [P, G, T, P])
        o_n = lnx
        tF = sb("tF", [P, G, GT])
        tH = sb("tH", [P, G, 2, GT], F16)
        tL = sb("tL", [P, G, 2, GT], F16)
        QS = sb("QS", [P, G, QUADS, GT], F16)
        T1 = sb("T1", [P, 2, GT], F16)
        kbs = sb("kbs", [P, 2, QUADS, 4, S], F16)
        KBX = sb("KBX", [P, QUADS, B, 4, SC], F16)
        VBX = [sb("VBXh", [P, 2, B, H // 2, 2 * DV], F16), sb("VBXl", [P, 2, B, H // 2, 2 * DV], F16)]
        VS = [sb("VSh", [P, G, T, H, DV], F16), sb("VSl", [P, G, T, H, DV], F16)]
        MX = sb("MX", [P, B, 2, H])
        MP = sb("MP", [P, B, 2, P], BF16)
        MT = sb("MT", [P, B, S], BF16)
        pr = sb("pr", [P, G, 2, GT])
        prh = sb("prh", [P, G, NPV, GT], F16)
        prl = sb("prl", [P, G, NPV, GT], F16)
        rec = sb("rec", [P, 2, H])
        lg = sb("lg", [P, T, 8])
        zz = sb("zz", [P, T, 8])
        ex = sb("ex", [P, T, 8])
        m8 = sb("m8", [P, T, 8])
        i8 = sb("i8", [P, T, 8], U32)
        i8f = sb("i8f", [P, T, 8])
        sel = sb("sel", [P, 2, T, 8])
        r1 = sb("r1", [P, T, 1])
        r2 = sb("r2", [P, T, 1])
        wt = sb("wt", [P, 2, G, T, 8])
        hr = sb("hr", [P, G, 2, GT])
        KS = [hr[:, g].rearrange("p a k -> p (a k)").bitcast(F16).rearrange("p (j k) -> p j k", j=QUADS) for g in range(G)]
        braw = hr[:, 0]
        bsl = prl[:, 1, 0:2, :]
        ones = prh[:, 1, 0, :]
        cx = lni[:, 0, 0:2, :]
        vtmp = lni[:, 1].rearrange("p t d -> p (t d)")
        hh, hhi, hlo = pr, prh, prl

        ps = [stk.enter_context(nc.psum_tensor(f"ps{i}", [P, GT], F32)) for i in range(8)]

        in_ctx, in_cst, in_x, in_small = sem("in_ctx"), sem("in_cst"), sem("in_x"), sem("in_small")
        in_w, out_done = [sem("in_w0"), sem("in_w1")], sem("out_done")
        zeroed, xb_ready = sem("zeroed"), sem("xb_ready")
        const_ready, bias_rows, bias_ready = sem("const_ready"), sem("bias_rows"), sem("bias_ready")
        ctx_turned, ctx_high, ctx_ready = sem("ctx_turned"), sem("ctx_high"), sem("ctx_ready")
        vctx_mm, vctx_ready = sem("vctx_mm"), sem("vctx_ready")
        w_high, w_ready = sem("w_high"), sem("w_ready")
        stack_mm, stack_high, stack_ready = sem("stack_mm"), sem("stack_high"), sem("stack_ready")
        ln_stat, ln_rstd, ln_done = sem("ln_stat"), sem("ln_rstd"), sem("ln_done")
        turn_mm, turn_first, turn_ready = sem("turn_mm"), sem("turn_first"), sem("turn_ready")
        kb_ready = sem("kb_ready")
        max_mm, max_read, neg_ready = sem("max_mm"), sem("max_read"), sem("neg_ready")
        neg_mm, negT_ready = sem("neg_mm"), sem("negT_ready")
        sc_mm, pr_ready, prh_ready, prl_ready, pv_done = (sem("sc_mm"), sem("pr_ready"), sem("prh_ready"),
                                                          sem("prl_ready"), sem("pv_done"))
        o_ready = sem("o_ready")
        sq_mm, sq_read = sem("sq_mm"), sem("sq_read")
        g0_mm, g0_lg, g0_exp, g0_ready = sem("g0_mm"), sem("g0_lg"), sem("g0_exp"), sem("g0_ready")
        g1_mm, g1_lg, g1_sub, g1_exp, g1_ready = sem("g1_mm"), sem("g1_lg"), sem("g1_sub"), sem("g1_exp"), sem("g1_ready")
        up_mm, act_ready, hid_ready, hi_ready, lo_ready, down_mm, down_read = (
            sem("up_mm"), sem("act_ready"), sem("hid_ready"), sem("hi_ready"), sem("lo_ready"), sem("down_mm"),
            sem("down_read"))
        add_read = sem("add_read")
        dve_step, pool_step = sem("dve_step"), sem("pool_step")

        ident = cst[:, CONST["ident"]:CONST["ident"] + P]
        sign = {n: cst[:, CONST["signs"] + i:CONST["signs"] + i + 1]
                for i, n in enumerate(["qa", "qb", "ka", "kb", "ba", "bb"])}
        iota = cst[:, CONST["iota"]:CONST["iota"] + 8]

        def row(name):
            i = ROWS.index(name)
            return rowb[:, i * P:(i + 1) * P]

        def rows4(name):
            return row(name).unsqueeze(1).broadcast_to([P, T, P])

        def weight(piece, col):
            o = sum(USED[:piece]) + col
            return wh[:, o:o + P], wl[:, o:o + P]

        LN = {"x0": (X, lnx, 1e-5, None), "x1": (X, lnx, 1e-5, None), "x2": (X, lni, 1e-5, None),
              "a": (act, lnx, 1e-6, ("g1", "b1")), "c": (act, lnx, 1e-6, ("g2", "b2")),
              "f": (act, act, 1e-6, ("g3", "b3")), "x3": (X, lnx, 1e-5, None)}
        TURN = {"x0": (lnx, 0), "o0": (o_n, 1), "x1": (lnx, 0), "x2": (lni, 0), "o1": (o_n, 1),
                "a": (lnx, 0), "o2": (o_n, 1), "c": (lnx, 0), "x3": (lnx, 0)}
        STACK_OF = {"q0": "x0", "q1": "x2", "k1": "x2", "q2": "a"}
        SCALE = [float(D) ** -0.5, float(S) ** -0.5, float(SC) ** -0.5]
        last_unit = {0: 3, 1: 15, 2: 3}

        block = stk.enter_context(nc.Block())

        @block.sync
        def _(sp):
            def piece(i):
                if i >= 2:
                    sp.wait_ge(w_ready, i - 1)
                sp.dma_start(wraw[:, i % 2, 0:USED[i]], weights[:, sum(USED[:i]):sum(USED[:i + 1])]).then_inc(in_w[i % 2], 16)

            sp.dma_start(cx, ctx.rearrange("(t p) d -> p t d", p=P)).then_inc(in_ctx, 16)
            sp.dma_start(cst[:], const).then_inc(in_cst, 16)
            piece(0)
            sp.dma_start(X[:], x.rearrange("(g t p) d -> p g t d", g=G, p=P)).then_inc(in_x, 16)
            sp.wait_ge(zeroed, 1)
            for r in range(2):
                sp.dma_start(braw[r:r + 1, :, :], qkbias).then_inc(bias_rows, 16)
            sp.dma_start(rowb[:], rows.partition_broadcast(P)).then_inc(in_small, 16)
            sp.dma_start(wg[:], gates).then_inc(in_small, 16)
            for i in range(1, PIECES):
                piece(i)
            for e in ev:
                if e[0] == "store":
                    g = e[1]
                    sp.wait_ge(add_read, nth[("add1", E1 - 1, g)])
                    sp.dma_start(out.rearrange("(g t p) d -> p g t d", g=G, p=P)[:, g], X[:, g]).then_inc(out_done, 16)
            sp.wait_ge(out_done, 16 * G)

        @block.gpsimd
        def _(pool):
            step = [0]

            def link(ins):
                step[0] += 1
                ins.then_inc(pool_step, 1)
                pool.wait_ge(pool_step, step[0])

            nc.gpsimd.memset(braw, 0.0).then_inc(zeroed, 1)
            nc.gpsimd.memset(neghalf[:], -0.5).then_inc(zeroed, 1)
            for v in VBX:
                nc.gpsimd.memset(v[:], 0.0).then_inc(zeroed, 1)
            nc.gpsimd.memset(MP[:], 0.0).then_inc(zeroed, 1)
            pool.wait_ge(zeroed, 5)
            nc.gpsimd.memset(VBX[0][0:64, :, :, :, D:DV], 1.0).then_inc(zeroed, 1)
            pool.wait_ge(zeroed, 6)
            nc.gpsimd.memset(VBX[0][64:128, :, :, :, D + DV:2 * DV], 1.0).then_inc(zeroed, 1)
            pool.wait_ge(zeroed, 7)
            nc.gpsimd.memset(VS[0][:, :, :, :, D:DV], 1.0).then_inc(zeroed, 1)
            nc.gpsimd.memset(VS[1][:, :, :, :, D:DV], 0.0).then_inc(zeroed, 1)
            pool.wait_ge(in_x, 16)
            pool.wait_ge(in_small, 32)
            for g in range(G):
                nc.gpsimd.tensor_tensor(act[:, g], X[:, g], rows4("bo"), ALU.add).then_inc(xb_ready, 1)
            nc.gpsimd.memset(kbs[:, 0], 0.0).then_inc(zeroed, 1)
            nc.gpsimd.memset(kbs[:, 1], 0.0).then_inc(zeroed, 1)
            for e in ev:
                kind, n = e[0], nth[e]
                if kind == "ln_stats":
                    k = n - 1
                    pool.wait_ge(ln_stat, n)
                    link(nc.gpsimd.tensor_scalar(rstd[:, k, :], mv[:, k, :, 1], LN[e[1]][2], None, ALU.add))
                    nc.gpsimd.tensor_tensor(rstd[:, k, :], rstd[:, k, :], neghalf[:], ALU.pow).then_inc(ln_rstd, 1)
                elif kind == "split" and e[1] > 0:
                    i = e[1]
                    pool.wait_ge(w_high, n)
                    cols = slice(sum(USED[:i]), sum(USED[:i + 1]))
                    nc.gpsimd.tensor_tensor(wl[:, cols], wraw[:, i % 2, 0:USED[i]], wh[:, cols],
                                            ALU.subtract).then_inc(w_ready, 1)
                elif kind == "hi":
                    _, l, g, x_, c = e
                    pool.wait_ge(hi_ready, n)
                    k = x_ if l == 0 else CH * x_ + c
                    if k >= NPV:
                        pool.wait_ge(down_mm, nth[("down", l, g, x_ - NPV, 0) if l == 0 else
                                                  ("down", l, g, (k - NPV) // CH, (k - NPV) % CH)])
                    nc.gpsimd.tensor_tensor(hlo[:, g, k % NPV, :], hh[:, g, buffer[("up",) + e[1:]], :], hhi[:, g, k % NPV, :],
                                            ALU.subtract).then_inc(lo_ready, 1)

        @block.tensor
        def _(pe):
            emptied = {}
            split_seen = [0]

            def take(b, read_signal, value):
                if b in emptied:
                    pe.wait_ge(*emptied[b])
                emptied[b] = (read_signal, value)

            def need_piece(i):
                if i + 1 > split_seen[0]:
                    pe.wait_ge(w_ready, i + 1)
                    split_seen[0] = i + 1

            def split_mm(o, a, b, start=True, stop=True, **kw):
                nc.tensor.matmul(o, a[0], b[0], start=start, stop=False, **kw)
                nc.tensor.matmul(o, a[0], b[1], start=False, stop=False, **kw)
                return nc.tensor.matmul(o, a[1], b[0], start=False, stop=stop, **kw)

            pe.wait_ge(in_cst, 16)
            for e in ev:
                kind, n = e[0], nth[e]
                o = ps[bank[e]] if e in bank else None
                if kind == "ctx":
                    pe.wait_ge(in_ctx, 16)
                    take(bank[e], ctx_ready, 1)
                    for t in range(2):
                        mm = nc.tensor.transpose(o[:, t * P:(t + 1) * P], cx[:, t, :], ident)
                    mm.then_inc(ctx_turned, 1)
                elif kind == "vctx":
                    need_piece(WEIGHTS[f"v{e[1]}"][0])
                    take(bank[e], vctx_ready, n)
                    for b in range(B):
                        both = [v[:, b, :, :].rearrange("p a k -> p (a k)") for v in cxt]
                        mm = split_mm(o[:, b * P:(b + 1) * P], both, weight(*WEIGHTS[f"v{e[1]}"]))
                    mm.then_inc(vctx_mm, 1)
                elif kind == "stack":
                    _, name, g, j = e
                    piece, col = WEIGHTS[name]
                    need_piece(piece)
                    if name in ("k0", "k2"):
                        src, width = [v[:] for v in cxs], B * SC
                        if n == 1:
                            pe.wait_ge(ctx_ready, 3)
                    else:
                        src, width = [tH[:, g, 0, :], tL[:, g, 0, :]], GT
                        if j == 0:
                            pe.wait_ge(turn_ready, nth[("turn", STACK_OF[name], g)])
                    take(bank[e], stack_ready, n)
                    biased = name in ("q0", "k0")
                    mm = split_mm(o[:, 0:width], weight(piece, col + j * P), src, stop=not biased)
                    if biased:
                        if n == 1:
                            pe.wait_ge(bias_ready, 1)
                            pe.wait_ge(const_ready, 5)
                        mm = nc.tensor.matmul(o[:, 0:width], bsl[:, 0 if name == "q0" else 1, j * P:(j + 1) * P],
                                              ones[:, 0:width], start=False, stop=True)
                    mm.then_inc(stack_mm, 1)
                elif kind == "turn":
                    _, name, g = e
                    src = TURN[name][0]
                    if name[:1] == "o":
                        pe.wait_ge(o_ready, nth[("out_norm", int(name[1]), 2 * g + 1)])
                    else:
                        pe.wait_ge(ln_done, nth[("ln_norm", name, g)])
                    take(bank[e], turn_ready, n)
                    for t in range(T):
                        mm = nc.tensor.transpose(o[:, t * P:(t + 1) * P], src[:, g, t, :], ident)
                    mm.then_inc(turn_mm, 1)
                elif kind == "square":
                    _, name, g = e
                    slot = 1 if name[:1] == "o" else 0
                    need_piece(WEIGHTS[name][0])
                    pe.wait_ge(turn_ready, nth[("turn", {"v1": "x2", "f": "c"}.get(name, name), g)])
                    take(bank[e], sq_read, n)
                    for t in range(T):
                        tt = slice(t * P, (t + 1) * P)
                        mm = split_mm(o[:, tt], (tH[:, g, slot, tt], tL[:, g, slot, tt]), weight(*WEIGHTS[name]))
                    mm.then_inc(sq_mm, 1)
                elif kind == "max":
                    _, a, b, u = e
                    g = b // 2
                    take(bank[e], max_read, n)
                    q0 = (b % 2) * S
                    if a != 1:
                        if u == 0:
                            pe.wait_ge(stack_ready, nth[("stack", f"q{a}", g, QUADS - 1)])
                            pe.wait_ge(stack_ready, nth[("stack", f"k{a}", 0, QUADS - 1)])
                        qt, half = u // 2, u % 2
                        for i in range(2):
                            j = 2 * half + i
                            mm = nc.tensor.matmul(o[:, i * S:(i + 1) * S], QS[:, g, j, q0 + qt * P:q0 + (qt + 1) * P],
                                                  KBX[:, j, b, :, :].rearrange("p h k -> p (h k)"), start=True, stop=True)
                    else:
                        if u == 0:
                            pe.wait_ge(kb_ready, nth[("kblocks", 1, b)])
                            pe.wait_ge(stack_ready, nth[("stack", "q1", g, QUADS - 1)])
                        kb = kbs[:, b % 2]
                        if u < 4:
                            v, heads = o[:].rearrange("p (h k) -> p h k", h=4), 4
                            nc.tensor.matmul(v, QS[:, g, u, q0:q0 + P], kb[:, u, :, 0:P], start=True, stop=True)
                        else:
                            j, h0 = (u - 4) // 2, 2 * ((u - 4) % 2)
                            v, heads = o[:].rearrange("p (h k) -> p h k", h=2), 2
                            nc.tensor.matmul(v, QS[:, g, j, q0 + P:q0 + 2 * P], kb[:, j, h0:h0 + 2, :], start=True,
                                             stop=True)
                            v = v[:, :, P:2 * P]
                        mm = nc.tensor.matmul(v, identb[:], trib[:, 0, :].unsqueeze(1).broadcast_to([P, heads, P]),
                                              start=False, stop=True, skip_group_check=True)
                    mm.then_inc(max_mm, 1)
                elif kind == "negmax":
                    pe.wait_ge(neg_ready, n)
                    take(bank[e], negT_ready, n)
                    for t in range(2):
                        mm = nc.tensor.matmul(o[:, t * P:(t + 1) * P], MP[:, e[2], t, :], identb[:], start=True, stop=True)
                    mm.then_inc(neg_mm, 1)
                elif kind == "scores":
                    _, a, b, u = e
                    g = b // 2
                    if u == 0:
                        pe.wait_ge(negT_ready, nth[("negmax", a, b)])
                        pe.wait_ge(const_ready, 5)
                    take(bank[e], prh_ready, n)
                    q0 = (b % 2) * S
                    mt = MT[:, b, :]
                    if a != 1:
                        for i in range(2):
                            p = 2 * u + i
                            nc.tensor.matmul(o[:, i * S:(i + 1) * S],
                                             KBX[:, p // 2, b, 2 * (p % 2):2 * (p % 2) + 2, :].rearrange("p h k -> p (h k)"),
                                             QS[:, g, p // 2, q0:q0 + S], start=True, stop=False)
                            mm = nc.tensor.matmul(o[:, i * S:(i + 1) * S],
                                                  pairsel[:, 2 * p:2 * p + 2, :].rearrange("p h k -> p (h k)"), mt,
                                                  start=False, stop=True)
                    else:
                        kb = kbs[:, b % 2]
                        j, h = u // 4, u % 4
                        kw = dict(start=False, stop=True, skip_group_check=True)
                        nc.tensor.matmul(o[:, 0:S], kb[:, j, h, 0:P], QS[:, g, j, q0:q0 + S], start=True, stop=True)
                        nc.tensor.matmul(o[:, S:S + P], kb[:, j, h, P:2 * P], QS[:, g, j, q0 + P:q0 + S], **kw)
                        nc.tensor.matmul(o[:, 0:S], headsel[:, u, :], mt, **kw)
                        nc.tensor.matmul(o[:, S:S + P], headsel[:, u, :], mt[:, P:S], **kw)
                        for c in (0, S):
                            mm = nc.tensor.matmul(o[:, c:c + P], identb[:], trib[:, 1, :], **kw)
                    mm.then_inc(sc_mm, 1)
                elif kind == "pv":
                    _, a, b, u = e
                    g = b // 2
                    pe.wait_ge(prl_ready, nth[("plow", a, b, u)])
                    if u == 0:
                        take(bank[e], o_ready, nth[("out_norm", a, b)])
                        if a == 1:
                            pe.wait_ge(sq_read, nth[("square", "v1", g)])
                        else:
                            pe.wait_ge(vctx_ready, a // 2 + 1)
                    ph, pl = prh[:, g, u % NPV, :], prl[:, g, u % NPV, :]
                    if a != 1:
                        for i in range(2):
                            p = 2 * u + i
                            for qt in range(2):
                                c = qt * H * DV + p * 2 * DV
                                cc = slice(i * S + qt * P, i * S + (qt + 1) * P)
                                mm = split_mm(o[:, c:c + 2 * DV], (ph[:, cc], pl[:, cc]),
                                              [v[:, a // 2, b, p, :] for v in VBX])
                    else:
                        t0 = 2 * (b % 2)
                        c = u * DV
                        v0 = [v[:, g, t0, u, :] for v in VS]
                        v1 = [v[:, g, t0 + 1, u, :] for v in VS]
                        split_mm(o[:, c:c + DV], (ph[:, 0:P], pl[:, 0:P]), v0)
                        c += H * DV
                        split_mm(o[:, c:c + DV], (ph[:, P:2 * P], pl[:, P:2 * P]), v0, stop=False)
                        mm = split_mm(o[:, c:c + DV], (ph[:, S:S + P], pl[:, S:S + P]), v1, start=False)
                    mm.then_inc(pv_done, 1)
                elif kind in ("gate0", "gate1"):
                    g = e[1]
                    l = 0 if kind == "gate0" else 1
                    pe.wait_ge(in_small, 32)
                    pe.wait_ge(turn_first, nth[("turn", "x1" if l == 0 else "x3", g)])
                    take(bank[e], (g0_lg, g1_lg)[l], n)
                    for t in range(T):
                        mm = nc.tensor.matmul(o[:, t * 8:(t + 1) * 8], tF[:, g, t * P:(t + 1) * P], wg[:, l, :],
                                              start=True, stop=True)
                    mm.then_inc((g0_mm, g1_mm)[l], 1)
                elif kind == "up":
                    _, l, g, x_, c = e
                    tt = (tH[:, g, 0, :], tL[:, g, 0, :])
                    pe.wait_ge(turn_ready, nth[("turn", "x1" if l == 0 else "x3", g)])
                    if l == 0:
                        need_piece(2)
                        take(bank[e], act_ready, n)
                        mm = split_mm(o[:], weight(1, x_ * P), tt)
                    else:
                        need_piece(FIRST1 + x_)
                        take(bank[e], hid_ready, n)
                        take(bank[e] + 1, act_ready, n)
                        split_mm(o[:], weight(FIRST1 + x_, c * P), tt)
                        mm = split_mm(ps[bank[e] + 1][:], weight(FIRST1 + x_, HID + c * P), tt)
                    mm.then_inc(up_mm, 1)
                elif kind == "down":
                    _, l, g, x_, c = e
                    pe.wait_ge(lo_ready, nth[("hi",) + e[1:]])
                    k = (x_ if l == 0 else CH * x_ + c) % NPV
                    if l == 0:
                        take(bank[e], down_read, nth_down0[e])
                        w = weight(2, x_ * P)
                    else:
                        if c == 0:
                            take(bank[e], add_read, nth[("add1", x_, g)])
                        w = weight(FIRST1 + x_, 2 * HID + c * P)
                    for t in range(T):
                        tt = slice(t * P, (t + 1) * P)
                        hparts = (hhi[:, g, k, tt], hlo[:, g, k, tt])
                        if l == 0:
                            mm = split_mm(o[:, tt], hparts, w)
                        else:
                            mm = split_mm(o[:, tt], hparts, w, start=(c == 0 and t == 0), stop=(c == CH - 1),
                                          skip_group_check=True)
                    mm.then_inc(down_mm, 1)

        @block.scalar
        def _(sc):
            for e in ev:
                kind, n = e[0], nth[e]
                src = ps[bank[e]] if e in bank else None
                if kind == "ctx":
                    sc.wait_ge(ctx_turned, 1)
                    nc.scalar.copy(cxs[0][:], src[:, 0:B * SC]).then_inc(ctx_high, 1)
                elif kind == "stack":
                    _, name, g, j = e
                    width = B * SC if name in ("k0", "k2") else GT
                    sc.wait_ge(stack_mm, n)
                    if n > 2:
                        sc.wait_ge(stack_ready, n - 2)
                    nc.scalar.activation(T1[:, n % 2, 0:width], src[:, 0:width], ACT.Copy,
                                         scale=sign[name[0] + "b"]).then_inc(stack_high, 1)
                elif kind == "turn":
                    _, name, g = e
                    sc.wait_ge(turn_mm, n)
                    dst = tF[:, g, :] if name in ("x1", "x3") else tH[:, g, TURN[name][1], :]
                    nc.scalar.copy(dst, src[:]).then_inc(turn_first, 1)
                elif kind == "negmax":
                    sc.wait_ge(neg_mm, n)
                    nc.scalar.copy(MT[:, e[2], :], src[:, 0:S]).then_inc(negT_ready, 1)
                elif kind == "scores":
                    _, a, b, u = e
                    g = b // 2
                    sc.wait_ge(sc_mm, n)
                    if e in nth_plow_before:
                        sc.wait_ge(prl_ready, nth_plow_before[e])
                    width = GT if a != 1 else S + P
                    nc.scalar.activation(pr[:, g, buffer[e], 0:width], src[:, 0:width], ACT.Exp,
                                         scale=SCALE[a]).then_inc(pr_ready, 1)
                    if u >= NPV:
                        sc.wait_ge(pv_done, nth[("pv", a, b, u - NPV)])
                    elif nth_pv_before[e]:
                        sc.wait_ge(pv_done, nth_pv_before[e])
                    nc.scalar.activation(prh[:, g, u % NPV, 0:width], src[:, 0:width], ACT.Exp,
                                         scale=SCALE[a]).then_inc(prh_ready, 1)
                elif kind == "gate0":
                    sc.wait_ge(g0_lg, n)
                    nc.scalar.activation(ex[:], lg[:], ACT.Exp, scale=-1.0).then_inc(g0_exp, 1)
                elif kind == "gate1":
                    sc.wait_ge(g1_sub, n)
                    nc.scalar.activation(ex[:], zz[:], ACT.Exp).then_inc(g1_exp, 1)
                elif kind == "up":
                    sc.wait_ge(up_mm, n)
                    if e in nth_up_before:
                        sc.wait_ge(hid_ready, nth_up_before[e])
                    if e[1] == 0:
                        nc.scalar.activation(hr[:, e[2], buffer[e], :], src[:], ACT.Relu).then_inc(act_ready, 1)
                    else:
                        nc.scalar.activation(hr[:, e[2], buffer[e], :], ps[bank[e] + 1][:], ACT.Silu).then_inc(act_ready, 1)
                elif kind == "hi":
                    _, l, g, x_, c = e
                    m = nth[("up",) + e[1:]]
                    sc.wait_ge(hid_ready, m)
                    k = x_ if l == 0 else CH * x_ + c
                    if k >= NPV:
                        sc.wait_ge(down_mm, nth[("down", l, g, x_ - NPV, 0) if l == 0 else
                                                ("down", l, g, (k - NPV) // CH, (k - NPV) % CH)])
                    nc.scalar.copy(hhi[:, g, k % NPV, :], hh[:, g, buffer[("up",) + e[1:]], :]).then_inc(hi_ready, 1)

        @block.vector
        def _(dve):
            step = [0]

            def link(ins):
                step[0] += 1
                ins.then_inc(dve_step, 1)
                dve.wait_ge(dve_step, step[0])

            dve.wait_ge(in_cst, 16)
            nc.vector.tensor_copy(identb[:], ident).then_inc(const_ready, 1)
            nc.vector.memset(ones, 1.0).then_inc(const_ready, 1)
            for e in ev:
                kind, n = e[0], nth[e]
                src = ps[bank[e]] if e in bank else None
                if kind == "bias":
                    dve.wait_ge(zeroed, 9)
                    dve.wait_ge(bias_rows, 32)
                    hi = T1[:]
                    link(nc.vector.tensor_scalar(hi, braw, sign["bb"], None, ALU.mult))
                    nc.vector.scalar_tensor_tensor(bsl, braw, sign["ba"], hi, ALU.mult,
                                                   ALU.add).then_inc(bias_ready, 1)
                    nc.vector.memset(KBX[:].bitcast(U32), 0)
                    nc.vector.tensor_copy(trib[:].rearrange("p a k -> p (a k)"),
                                          cst[:, CONST["tri_q"]:CONST["tri_q"] + 2 * P]).then_inc(const_ready, 1)
                    heads = cst[:, CONST["heads"]:CONST["heads"] + H].unsqueeze(2)
                    nc.vector.tensor_copy(pairsel[:], heads.broadcast_to([P, H, SC])).then_inc(const_ready, 1)
                    nc.vector.tensor_copy(headsel[:], heads.broadcast_to([P, H, P])).then_inc(const_ready, 1)
                elif kind == "split":
                    i = e[1]
                    cols = slice(sum(USED[:i]), sum(USED[:i + 1]))
                    raw, hi, lo = wraw[:, i % 2, 0:USED[i]], wh[:, cols], wl[:, cols]
                    dve.wait_ge(in_w[i % 2], 16 * (i // 2 + 1))
                    nc.vector.tensor_copy(hi, raw).then_inc(w_high, 1)
                    if i == 0:
                        dve.wait_ge(w_high, 1)
                        nc.vector.tensor_tensor(lo, raw, hi, ALU.subtract).then_inc(w_ready, 1)
                elif kind == "ctx":
                    dve.wait_ge(ctx_high, 1)
                    nc.vector.tensor_tensor(cxs[1][:], src[:, 0:B * SC], cxs[0][:], ALU.subtract).then_inc(ctx_ready, 1)
                    dve.wait_ge(ctx_ready, 1)
                    for i in range(2):
                        nc.vector.tensor_copy(cxt[i][:], cxs[i][:].rearrange("p (b k) -> p b k", b=B).unsqueeze(2)
                                              .broadcast_to([P, B, 2, SC])).then_inc(ctx_ready, 1)
                elif kind == "vctx":
                    dve.wait_ge(vctx_mm, n)
                    dve.wait_ge(zeroed, 9)
                    dve.wait_ge(in_small, 32)
                    if e[1] == 0:
                        link(nc.vector.tensor_tensor(vtmp.rearrange("p (b d) -> p b d", b=B),
                                                     src[:].rearrange("p (b d) -> p b d", b=B),
                                                     row("bv").unsqueeze(1).broadcast_to([P, B, P]), ALU.add))
                    else:
                        link(nc.vector.tensor_copy(vtmp, src[:]))
                    for half in range(2):
                        pp = slice(64 * half, 64 * half + 64)
                        v = vtmp[pp, :].rearrange("p (be two d) -> p be two d", two=2, d=D)[:, :, half, :]
                        dst = [t[pp, e[1] // 2].rearrange("p b e (two d) -> p (b e) two d", two=2)[:, :, half, 0:D] for t in VBX]
                        link(nc.vector.tensor_copy(dst[0], v))
                        ins = nc.vector.tensor_tensor(dst[1], v, dst[0], ALU.subtract)
                    ins.then_inc(vctx_ready, 1)
                elif kind == "stack":
                    _, name, g, j = e
                    width = B * SC if name in ("k0", "k2") else GT
                    dve.wait_ge(stack_high, n)
                    t1 = T1[:, n % 2, :]
                    sa = sign[name[0] + "a"]
                    if name in ("k0", "k2"):
                        for h in range(4):
                            pp = slice(SLOT * h, SLOT * (h + 1))
                            ins = nc.vector.scalar_tensor_tensor(
                                KBX[pp, j, :, h, :], src[pp, 0:width].rearrange("p (b k) -> p b k", b=B), sa[pp, :],
                                t1[pp, 0:width].rearrange("p (b k) -> p b k", b=B), ALU.mult, ALU.add)
                    else:
                        dst = QS[:, g, j, :] if name[:1] == "q" else KS[g][:, j, :]
                        ins = nc.vector.scalar_tensor_tensor(dst, src[:], sa, t1, ALU.mult, ALU.add)
                    ins.then_inc(stack_ready, 1)
                elif kind == "turn":
                    _, name, g = e
                    slot = TURN[name][1]
                    dve.wait_ge(turn_first, n)
                    whole = src[:]
                    if name in ("x1", "x3"):
                        whole = tF[:, g, :]
                        link(nc.vector.tensor_copy(tH[:, g, slot, :], whole))
                    nc.vector.tensor_tensor(tL[:, g, slot, :], whole, tH[:, g, slot, :], ALU.subtract).then_inc(turn_ready, 1)
                elif kind == "kblocks":
                    b = e[2]
                    dve.wait_ge(zeroed, 11)
                    dve.wait_ge(stack_ready, nth[("stack", "k1", b // 2, QUADS - 1)])
                    if b >= 2:
                        dve.wait_ge(sc_mm, nth[("scores", 1, b - 2, 15)])
                    for h in range(4):
                        pp = slice(SLOT * h, SLOT * (h + 1))
                        ins = nc.vector.tensor_copy(kbs[pp, b % 2, :, h, :], KS[b // 2][pp, :, (b % 2) * S:(b % 2) * S + S])
                    ins.then_inc(kb_ready, 1)
                elif kind == "ln_stats":
                    _, name, g = e
                    from_ = LN[name][0]
                    if name == "x0":
                        dve.wait_ge(in_x, 16)
                    for t in range(T):
                        ins = nc.vector.bn_stats(stat[:, t, :], from_[:, g, t, :])
                    link(ins)
                    for t in range(T):
                        ins = nc.vector.bn_aggr(mv[:, n - 1, t, :], stat[:, t, :])
                    ins.then_inc(ln_stat, 1)
                elif kind == "ln_norm":
                    _, name, g = e
                    from_, dst, _, affine = LN[name]
                    k = nth[("ln_stats", name, g)] - 1
                    dve.wait_ge(ln_rstd, k + 1)
                    for t in range(T):
                        ins = nc.vector.tensor_scalar(dst[:, g, t, :], from_[:, g, t, :], mv[:, k, t, 0:1], rstd[:, k, t:t + 1],
                                                      ALU.subtract, ALU.mult)
                    if affine:
                        link(ins)
                        link(nc.vector.tensor_tensor(dst[:, g], dst[:, g], rows4(affine[0]), ALU.mult))
                        ins = nc.vector.tensor_tensor(dst[:, g], dst[:, g], rows4(affine[1]), ALU.add)
                    if name == "f":
                        link(ins)
                        ins = nc.vector.tensor_tensor(X[:, g], X[:, g], act[:, g], ALU.add)
                    ins.then_inc(ln_done, 1)
                    dve.wait_ge(ln_done, n)
                elif kind == "max":
                    _, a, b, u = e
                    dve.wait_ge(max_mm, n)
                    if a != 1:
                        o, heads = MX[:, b, u // 2, 8 * (u % 2):8 * (u % 2) + 8], 8
                    elif u < 4:
                        o, heads = MX[:, b, 0, 4 * u:4 * u + 4], 4
                    else:
                        o, heads = MX[:, b, 1, 2 * (u - 4):2 * (u - 4) + 2], 2
                    nc.vector.tensor_reduce(o, src[:].rearrange("p (h k) -> p h k", h=heads), AX_X,
                                            ALU.max).then_inc(max_read, 1)
                elif kind == "negmax":
                    _, a, b = e
                    dve.wait_ge(max_read, nth[("max", a, b, 11 if a == 1 else 3)])
                    dve.wait_ge(zeroed, 9)
                    link(nc.vector.tensor_scalar(MP[:, b, :, 0:H], MX[:, b], -1.0, None, ALU.mult))
                    nc.vector.scalar_tensor_tensor(MP[:, b, :, H:2 * H], MX[:, b], -1.0, MP[:, b, :, 0:H], ALU.mult,
                                                   ALU.subtract).then_inc(neg_ready, 1)
                elif kind == "plow":
                    _, a, b, u = e
                    g, width = b // 2, (GT if a != 1 else S + P)
                    dve.wait_ge(prh_ready, nth[("scores", a, b, u)])
                    nc.vector.tensor_tensor(prl[:, g, u % NPV, 0:width], pr[:, g, buffer[("scores", a, b, u)], 0:width], prh[:, g, u % NPV, 0:width],
                                            ALU.subtract).then_inc(prl_ready, 1)
                elif kind == "out_norm":
                    _, a, b = e
                    g = b // 2
                    dve.wait_ge(pv_done, nth[("pv", a, b, last_unit[a])])
                    v = ps[4 + g][:, 0:2 * H * DV].rearrange("p (q h d) -> p q h d", q=2, d=DV)
                    link(nc.vector.reciprocal(rec[:], v[:, :, :, D]))
                    for q in range(2):
                        ins = nc.vector.tensor_tensor(
                            o_n[:, g, 2 * (b % 2) + q, :].rearrange("p (h d) -> p h d", d=D), v[:, q, :, 0:D],
                            rec[:, q, :].unsqueeze(2).broadcast_to([P, H, D]), ALU.mult)
                    ins.then_inc(o_ready, 1)
                elif kind == "square":
                    _, name, g = e
                    dve.wait_ge(sq_mm, n)
                    y = src[:].rearrange("p (t d) -> p t d", t=T)
                    if name == "o0":
                        dve.wait_ge(xb_ready, g + 1)
                        ins = nc.vector.tensor_tensor(X[:, g], y, act[:, g], ALU.add)
                    elif name == "v1":
                        v = src[:].rearrange("p (t h d) -> p t h d", t=T, d=D)
                        link(nc.vector.tensor_copy(VS[0][:, g, :, :, 0:D], v))
                        ins = nc.vector.tensor_tensor(VS[1][:, g, :, :, 0:D], v, VS[0][:, g, :, :, 0:D], ALU.subtract)
                    elif name == "o1":
                        link(nc.vector.tensor_tensor(act[:, g], y, rows4("bo1"), ALU.add))
                        ins = nc.vector.scalar_tensor_tensor(act[:, g], act[:, g], 0.0, lni[:, g], ALU.max, ALU.add)
                    elif name == "o2":
                        link(nc.vector.tensor_tensor(act[:, g], y, rows4("bo2"), ALU.add))
                        ins = nc.vector.tensor_scalar(act[:, g], act[:, g], 0.0, 2.0, ALU.max, ALU.mult)
                    else:
                        link(nc.vector.tensor_tensor(act[:, g], y, rows4("bf"), ALU.add))
                        ins = nc.vector.scalar_tensor_tensor(act[:, g], act[:, g], 0.0, lnx[:, g], ALU.max, ALU.add)
                    ins.then_inc(sq_read, 1)
                    dve.wait_ge(sq_read, n)
                elif kind == "gate0":
                    g = e[1]
                    dve.wait_ge(g0_mm, n)
                    nc.vector.tensor_copy(lg[:].rearrange("p t x -> p (t x)"), src[:, 0:8 * T]).then_inc(g0_lg, 1)
                    dve.wait_ge(g0_lg, n)
                    lb = rowb[:, len(ROWS) * P:len(ROWS) * P + 8]
                    link(nc.vector.tensor_tensor(zz[:], lg[:], lb.unsqueeze(1).broadcast_to([P, T, 8]), ALU.add))
                    for t in range(T):
                        ins = nc.vector.max(m8[:, t, :], zz[:, t, :])
                    link(ins)
                    for t in range(T):
                        ins = nc.vector.max_index(i8[:, t, :], m8[:, t, :], zz[:, t, :])
                    link(ins)
                    link(nc.vector.tensor_copy(i8f[:], i8[:]))
                    for k in range(2):
                        ins = nc.vector.tensor_tensor(sel[:, k], iota.unsqueeze(1).broadcast_to([P, T, 8]),
                                                      i8f[:, :, k:k + 1].broadcast_to([P, T, 8]), ALU.is_equal)
                    link(ins)
                    link(nc.vector.tensor_tensor(sel[:, 0], sel[:, 0], sel[:, 1], ALU.add))
                    dve.wait_ge(g0_exp, n)
                    link(nc.vector.tensor_scalar(zz[:], ex[:], 1.0, None, ALU.add))
                    link(nc.vector.reciprocal(zz[:], zz[:]))
                    link(nc.vector.tensor_tensor(zz[:], zz[:], sel[:, 0], ALU.mult))
                    link(nc.vector.tensor_reduce(r1[:], zz[:], AX_X, ALU.add))
                    link(nc.vector.tensor_scalar(r1[:], r1[:], 1e-6, None, ALU.add))
                    link(nc.vector.reciprocal(r2[:], r1[:]))
                    nc.vector.tensor_tensor(wt[:, 0, g], zz[:], r2[:].broadcast_to([P, T, 8]), ALU.mult).then_inc(g0_ready, 1)
                    dve.wait_ge(g0_ready, n)
                elif kind == "gate1":
                    g = e[1]
                    dve.wait_ge(g1_mm, n)
                    nc.vector.tensor_copy(lg[:].rearrange("p t x -> p (t x)"), src[:, 0:8 * T]).then_inc(g1_lg, 1)
                    dve.wait_ge(g1_lg, n)
                    link(nc.vector.tensor_reduce(r1[:], lg[:], AX_X, ALU.max))
                    nc.vector.tensor_tensor(zz[:], lg[:], r1[:].broadcast_to([P, T, 8]), ALU.subtract).then_inc(g1_sub, 1)
                    dve.wait_ge(g1_exp, n)
                    link(nc.vector.tensor_reduce(r1[:], ex[:], AX_X, ALU.add))
                    link(nc.vector.reciprocal(r2[:], r1[:]))
                    link(nc.vector.tensor_tensor(zz[:], ex[:], r2[:].broadcast_to([P, T, 8]), ALU.mult))
                    for t in range(T):
                        ins = nc.vector.max(m8[:, t, :], zz[:, t, :])
                    link(ins)
                    for t in range(T):
                        ins = nc.vector.max_index(i8[:, t, :], m8[:, t, :], zz[:, t, :])
                    link(ins)
                    link(nc.vector.tensor_copy(i8f[:], i8[:]))
                    link(nc.vector.tensor_tensor(sel[:, 0], iota.unsqueeze(1).broadcast_to([P, T, 8]),
                                                 i8f[:, :, 0:1].broadcast_to([P, T, 8]), ALU.is_equal))
                    link(nc.vector.tensor_tensor(sel[:, 0], sel[:, 0], m8[:, :, 0:1].broadcast_to([P, T, 8]), ALU.mult))
                    nc.vector.tensor_scalar(wt[:, 1, g], sel[:, 0], 2.0, None, ALU.mult).then_inc(g1_ready, 1)
                    dve.wait_ge(g1_ready, n)
                elif kind == "up":
                    dve.wait_ge(act_ready, n)
                    if e in nth_hi_before:
                        dve.wait_ge(lo_ready, nth_hi_before[e])
                    first = hr[:, e[2], buffer[e], :] if e[1] == 0 else src[:]
                    nc.vector.tensor_tensor(hh[:, e[2], buffer[e], :], first, hr[:, e[2], buffer[e], :], ALU.mult).then_inc(hid_ready, 1)
                elif kind == "down" and e[1] == 0:
                    _, _, g, x_, _ = e
                    dve.wait_ge(down_mm, n)
                    if x_ > 0:
                        dve.wait_ge(down_read, nth_down0[("down", 0, g, x_ - 1, 0)])
                    y = src[:].rearrange("p (t d) -> p t d", t=T)
                    if x_ == E0 - 1:
                        ins = nc.vector.tensor_tensor(X[:, g], y, X[:, g], ALU.add)
                    else:
                        for t in range(T):
                            ins = nc.vector.scalar_tensor_tensor(X[:, g, t, :], y[:, t, :], wt[:, 0, g, t, x_:x_ + 1],
                                                                 X[:, g, t, :], ALU.mult, ALU.add)
                    ins.then_inc(down_read, 1)
                    if x_ == E0 - 1:
                        dve.wait_ge(down_read, nth_down0[e])
                elif kind == "add1":
                    _, x_, g = e
                    dve.wait_ge(down_mm, nth[("down", 1, g, x_, CH - 1)])
                    if x_ > 0:
                        dve.wait_ge(add_read, nth[("add1", x_ - 1, g)])
                    y = ps[4 + g][:].rearrange("p (t d) -> p t d", t=T)
                    if x_ == 0:
                        ins = nc.vector.tensor_tensor(X[:, g], y, X[:, g], ALU.add)
                    else:
                        k = order(x_)
                        for t in range(T):
                            ins = nc.vector.scalar_tensor_tensor(X[:, g, t, :], y[:, t, :], wt[:, 1, g, t, k:k + 1],
                                                                 X[:, g, t, :], ALU.mult, ALU.add)
                    ins.then_inc(add_read, 1)


def _pack(inputs):
    f = {k: np.ascontiguousarray(v) for k, v in inputs.items()}

    def stack(w):
        w = w.reshape(w.shape[0], QUADS, 4, 1, D)
        w = np.concatenate([w, w, w, np.zeros_like(w)], axis=3)
        return w.reshape(w.shape[0], QUADS * P)

    def per_head(w):
        return w.transpose(1, 0, 2).reshape(P, P)

    const = np.zeros((P, NCONST), np.float32)
    const[:, 0:P] = np.eye(P)
    q, k = np.meshgrid(np.arange(P), np.arange(P), indexing="ij")
    const[:, P:2 * P] = np.where(k > q, NEG, 0.0)
    const[:, 2 * P:3 * P] = np.where(q > k, NEG, 0.0)
    third = (np.arange(P) % SLOT) // D
    for i, low in ((0, 2), (2, 1)):
        const[:, 384 + i] = third == low
        const[:, 385 + i] = np.where(third == low, -1.0, 1.0)
    const[:, 388] = np.arange(P) == 1
    const[:, 389] = np.where(np.arange(P) == 1, -1.0, 1.0)
    const[:, 390:398] = np.arange(8)
    const[:, 398:414] = (np.arange(P)[:, None] % H == np.arange(H)) & (np.arange(P)[:, None] < 2 * H)
    Wk, Wq = [f["L0_xattn_Wk"].T, per_head(f["L1_xattn_Wk1"]), per_head(f["L1_xattn_Wk2"])], [
        f["L0_xattn_Wq"].T, per_head(f["L1_xattn_Wq1"]), per_head(f["L1_xattn_Wq2"])]
    Wv = [f["L0_xattn_Wv"].T, per_head(f["L1_xattn_Wv1"]), per_head(f["L1_xattn_Wv2"])]
    Wo = [f["L0_xattn_Wo"].T, f["L1_xattn_Wo1"], f["L1_xattn_Wo2"]]
    weights = []
    for i in range(3):
        parts = [stack(Wk[i]), stack(Wq[i]), Wv[i], Wo[i]] + ([f["L1_xattn_Wf"]] if i == 2 else [])
        weights.append(np.concatenate(parts, axis=1))
    rows = np.concatenate([f[n] for n in (
        "L0_xattn_bv", "L0_xattn_bo", "L1_xattn_bo1", "L1_xattn_g1", "L1_xattn_b1", "L1_xattn_bo2", "L1_xattn_g2",
        "L1_xattn_b2", "L1_xattn_bf", "L1_xattn_g3", "L1_xattn_b3", "L0_ffn_lb_bias")])
    weights[1:1] = [
        np.concatenate([f["L0_ffn_w1"].transpose(2, 0, 1).reshape(P, -1), f["L0_ffn_cfc"].T], axis=1),
        np.concatenate([f["L0_ffn_w2"].transpose(2, 0, 1).reshape(P, -1), f["L0_ffn_cproj"].T], axis=1)]

    def down(w):
        return w.reshape(-1, CH, P, P).transpose(2, 0, 1, 3).reshape(P, -1, HID)

    w1 = np.concatenate([
        np.concatenate([f["L1_ffn_w_up"], f["L1_ffn_ws_up"][None]]).transpose(1, 0, 2),
        np.concatenate([f["L1_ffn_w_gate"], f["L1_ffn_ws_gate"][None]]).transpose(1, 0, 2),
        down(np.concatenate([f["L1_ffn_w_down"], f["L1_ffn_ws_down"][None]]))], axis=2)
    for n in range(E1):
        weights.append(w1[:, order(n)])
    return {
        "x": f["x"].reshape(-1, P), "ctx": f["ctx_1024"].reshape(-1, P), "const": const,
        "weights": np.concatenate(weights, axis=1),
        "qkbias": np.stack([stack(f["L0_xattn_bq"][None])[0], stack(f["L0_xattn_bk"][None])[0]])[None], "rows": rows,
        "gates": np.stack([f["L0_ffn_gate_w"].T, f["L1_ffn_w_router"]], axis=1),
    }


def kernel(**inputs):
    import concourse.bacc as _bacc
    from concourse.bass_utils import run_bass_kernel_spmd as _run

    nc = _bacc.Bacc("TRN2", target_bir_lowering=False, num_devices=1)
    arrays, args = {}, []
    for name, a in _pack({k: np.asarray(v) for k, v in inputs.items()}).items():
        a = np.ascontiguousarray(a)
        arrays[f"in_{name}"] = a
        args.append(nc.dram_tensor(f"in_{name}", a.shape, mybir.dt.from_np(a.dtype), kind="ExternalInput").ap())
    out = nc.dram_tensor("out", (B * S, P), F32, kind="ExternalOutput").ap()
    build(nc, *args, out)
    r = _run(nc, [arrays], core_ids=[0])
    return r.results[0]["out"].reshape(B, S, P)
```

```python
from contextlib import ExitStack

import numpy as np
import concourse.bass as bass
import concourse.mybir as mybir

ALU = mybir.AluOpType
ACT = mybir.ActivationFunctionType
F32 = mybir.dt.float32
F16 = mybir.dt.float16
BF16 = mybir.dt.bfloat16
U32 = mybir.dt.uint32
AX_X = mybir.AxisListType.X

P = 128
B, S, SC = 4, 256, 64
H, D = 16, 8
G, T = 2, 4
GT = T * P
QUADS, SLOT = 4, 32
E0 = 9
E1, HID, CH = 8, 512, 4
NEG = -1.0e30
DV = D + 1
NPV = 3

ROWS = ["bv", "bo", "bo1", "g1", "b1", "bo2", "g2", "b2", "bf", "g3", "b3"]
CONST = {"ident": 0, "tri_q": 128, "tri_k": 256, "signs": 384, "iota": 390, "heads": 398}
NCONST = 414
PIECE = 3 * HID
WEIGHTS = {}
for _a, _piece in enumerate((0, 3, 4)):
    WEIGHTS[f"k{_a}"] = (_piece, 0)
    WEIGHTS[f"q{_a}"] = (_piece, QUADS * P)
    WEIGHTS[f"v{_a}"] = (_piece, 2 * QUADS * P)
    WEIGHTS[f"o{_a}"] = (_piece, 2 * QUADS * P + P)
WEIGHTS["f"] = (4, 2 * QUADS * P + 2 * P)
WEIGHTS["up0"], WEIGHTS["down0"] = (1, 0), (2, 0)
FIRST1 = 5
PIECES = FIRST1 + E1
USED = [1280, 1152, 1152, 1280, 1408] + [PIECE] * E1

LAST = {0: 3, 1: 15, 2: 3}
GROUP_LEAD = 81.0
TABLE_LOAD = 1.3
LOAD = 5.0
ARRIVES = {"ctx": 4.5, ("split", 0): 5.5, "split": 14.0, ("ln_stats", "x0"): 8.0, "bo_add": 10.0, "kbs_zero": 7.0}
PRESSING = {
    "add1": -206, "down0": -311, "down1": -380, "gate0": -64, "gate1": 365, "hi0": -77, "hi1": -31,
    "kblocks": 1089, "ln_norm": 188, "ln_stats": 766, "lo0_dve": 11, "lo1": 37, "max": 108, "negmax": 313,
    "out_norm": 124, "plow": 600, "plow_pool": 560, "pv": 382, "scores": 108, "split": -40, "split_low":
    -286, "square": 785, "stack": 104, "turn": 157, "up0": -465, "up1": -843,
}
SHARED = 6
HOP = 0.13


def steps():
    after = {}

    def chain(seq, *first):
        prev = list(first)
        for e in seq:
            after.setdefault(e, []).extend(prev)
            prev = [e]
        return prev[0]

    def also(e, *before):
        after[e].extend(before)

    ctx = chain([("split", 0), ("ctx",), ("bias",)])
    k0 = chain([("stack", "k0", 0, j) for j in range(QUADS)], ctx)
    masks0 = chain([("masks0",)], ctx)
    masks1 = chain([("masks1",)], masks0)
    room = chain([("kbs_zero",)])
    v0 = chain([("vctx", 0)], k0)
    for i in range(1, PIECES):
        chain([("split", i)], ("split", i - 1), *([v0] if i == 1 else []))
        chain([("split_low", i, j) for j in range(3)], ("split", i), *([("split_low", i - 1, 2)] if i > 1 else []))
    k2 = chain([("stack", "k2", 0, j) for j in range(QUADS)], ("split_low", 4, 2), *[("scores", 0, b, 3) for b in range(B)])
    chain([("vctx", 2)], ("split_low", 4, 2))

    def attention(a, g, k, q):
        before, line = [k, q], []
        if a == 1:
            before += [masks1, room]
        for b in (2 * g, 2 * g + 1):
            if a == 1:
                before = [chain([("kblocks", 1, b)], *before)]
                if b >= 2:
                    also(("kblocks", 1, b), ("scores", 1, b - 2, 15))
            before = [chain([("max", a, b, u) for u in range(12 if a == 1 else 4)] + [("negmax", a, b)], *before)]
            line += [(a, b, u) for u in range(LAST[a] + 1)]
        for i, s in enumerate(line):
            chain([("scores", *s), plow(*s), ("pv", *s)])
            also(("scores", *s), ("negmax", a, s[1]), masks0)
            if i:
                for kind in ("scores", "pv"):
                    also((kind, *s), (kind, *line[i - 1]))
            if i >= 2:
                also(plow(*s), plow(*line[i - 2]))
            if s[2] == LAST[a]:
                chain([("out_norm", a, s[1])], ("pv", *s))
            if s[2] == 0:
                also(("pv", *s), ("square", "v1", g) if a == 1 else ("vctx", a))
                if s[1] % 2:
                    also(("pv", *s), ("out_norm", a, s[1] - 1))
        return chain([("turn", f"o{a}", g), ("square", f"o{a}", g)], ("out_norm", a, 2 * g + 1))

    def normed(name, g, *first):
        return chain([("ln_stats", name, g), ("ln_norm", name, g), ("turn", name, g)], *first)

    def experts(l, g, turned, gate):
        line = [(g, e, 0) for e in range(E0)] if l == 0 else [(g, e, c) for e in range(E1) for c in range(CH)]
        for i, s in enumerate(line):
            chain([(f"up{l}", *s), (f"hi{l}", *s), low_step(l, *s), (f"down{l}", *s)])
            also((f"up{l}", *s), turned, ("split_low", 2 if l == 0 else FIRST1 + s[1], 2))
            if i:
                for kind in ("up", "hi", "down"):
                    also((f"{kind}{l}", *s), (f"{kind}{l}", *line[i - 1]))
                also(low_step(l, *s), *[low_step(l, *x) for x in line[max(i - 2, 0):i]
                                        if low_step(l, *x)[0] == low_step(l, *s)[0]])
            elif l == 0:
                also(("down0", *s), gate)
            if l == 1 and s[2] == CH - 1:
                chain([("add1", g, s[1])], ("down1", *s), *([gate] if s[1] == 1 else []),
                      *([("add1", g, s[1] - 1)] if s[1] else []))
            if l == 1 and s[2] == 0 and s[1]:
                also(("down1", *s), ("add1", g, s[1] - 1))
        return ("down0", *line[-1]) if l == 0 else ("add1", g, E1 - 1)

    for g in range(G):
        chain([("bo_add", g)])
        e = normed("x0", g)
        e = chain([("stack", "q0", g, j) for j in range(QUADS)], e, ctx)
        e = attention(0, g, k0, e)
        also(e, ("bo_add", g))
        e = normed("x1", g, e)
        e = experts(0, g, e, chain([("gate0", g)], e))
        e = normed("x2", g, e)
        also(("ln_norm", "x2", g), ("vctx", 2))
        also(("turn", "x2", g), ("split_low", 3, 2))
        k = chain([("stack", "k1", g, j) for j in range(QUADS)], e)
        q = chain([("stack", "q1", g, j) for j in range(QUADS)], e)
        chain([("square", "v1", g)], e)
        e = attention(1, g, k, q)
        e = normed("a", g, e)
        e = chain([("stack", "q2", g, j) for j in range(QUADS)], e, k2)
        e = attention(2, g, k2, e)
        e = normed("c", g, e)
        e = chain([("square", "f", g), ("ln_stats", "f", g), ("ln_norm", "f", g)], e)
        e = normed("x3", g, e)
        experts(1, g, e, chain([("gate1", g)], e))
    return after


def plow(a, b, u):
    return ("plow" if u % 2 == 0 else "plow_pool", a, b, u)


def low_step(l, g, e, c):
    return ("lo0_dve" if l == 0 and e % 2 else f"lo{l}", g, e, c)


def parts(e):
    k = e[0]
    if k == "stack":
        return [("pe", .4), ("act", .4), ("dve", 1.2)] if e[1] in ("k0", "k2") else [("pe", .7), ("act", .6), ("dve", .7)]
    if k == "scores":
        return [("pe", .46), ("act", .75 if e[1] == 1 else .95)]
    if k == "max":
        return [("pe", .43 if e[1] == 1 else .22), ("dve", .6)]
    if k == "split":
        return [("dve", .8 if e[1] else 2.3)]
    if k == "ln_norm":
        return [("dve", {"a": 2.4, "c": 2.4, "f": 3.2}.get(e[1], 1.1))]
    if k == "plow":
        return [("dve", .47 if e[1] == 1 else .6)]
    return {"up0": [("pe", .65), ("act", 1.1)], "up1": [("pe", 1.3), ("act", .5), ("dve", .6)],
            "down0": [("pe", .67), ("act", 1.1), ("pool", 1.15)], "down1": [("pe", .67)],
            "split_low": [("pool", 1.05)], "plow_pool": [("pool", .85 if e[1:2] == (1,) else 1.15)], "hi0": [("act", .52)],
            "lo0": [("pool", 1.12)], "lo1": [("pool", 1.12)], "lo0_dve": [("dve", .62)],
            "turn": [("pe", .9), ("act", .5), ("dve", .8)], "square": [("pe", .7), ("dve", 1.3)],
            "negmax": [("dve", .3), ("pe", .15), ("act", .3)], "pv": [("pe", .25)], "out_norm": [("dve", .9)],
            "hi1": [("act", .52)], "add1": [("dve", 1.1)], "ln_stats": [("dve", 1.2), ("pool", 1.2)],
            "kblocks": [("dve", 1.35)], "gate0": [("pe", .9), ("dve", 4.)], "gate1": [("pe", .9), ("dve", 4.)],
            "ctx": [("pe", .9), ("act", .3), ("dve", .8)], "vctx": [("pe", .7), ("dve", 2.)], "bias": [("dve", 2.1)],
            "masks0": [("dve", .6)], "masks1": [("dve", 1.4)], "kbs_zero": [("pool", 3.6)], "bo_add": [("pool", 1.2)]}[k]


def group(e):
    if e[0] in ("kblocks", "max", "negmax", "scores", "plow", "plow_pool", "pv", "out_norm"):
        return e[2] // 2
    if e[0] in ("gate0", "gate1", "up0", "up1", "hi0", "hi1", "lo0", "lo1", "lo0_dve", "down0", "down1", "add1", "bo_add"):
        return e[1]
    return e[2] if e[0] != "split_low" and len(e) > 2 else 0


def reader(e):
    return 1 if e[0] in ("max", "scores", "up0", "up1", "gate0", "gate1", "down0") else len(parts(e)) - 1


def banks_of(e):
    if e[0] == "up1":
        return 2
    return int(e[0] in ("max", "scores", "up0", "ctx", "vctx", "stack", "turn", "square", "negmax", "gate0", "gate1",
                        "down0"))


def schedule():
    after = steps()
    stages = {e: parts(e) for e in after}
    behind, waiting = {e: [] for e in after}, {}
    for e, before in after.items():
        waiting[e] = len(set(before))
        for b in set(before):
            behind[b].append(e)
    frees, lines = {}, {}
    for e in after:
        if e[0] in ("scores", "up0", "up1"):
            lines.setdefault((e[0], group(e)), []).append(e)
    for (kind, _), line in lines.items():
        for i, e in enumerate(line):
            two, three = (line[i - 2][1:] if i >= 2 else None), (line[i - NPV][1:] if i >= NPV else None)
            if kind == "scores":
                frees[e, 1] = [(plow(*two), 0)] if two else []
                frees[e, 1] += [(("pv", *three), 0)] if three else []
            else:
                l = kind[-1]
                if two:
                    low = low_step(int(l), *two), 0
                    frees[e, 1] = [low] if l == "0" else [(("up1", *two), 2)]
                    frees[e, 2] = [low]
                frees[(f"hi{l}", *e[1:]), 0] = [((f"down{l}", *three), 0)] if three else []
                if l == "0" and two:
                    frees[("down0", *e[1:]), 1] = [(("down0", *two), 2)]
    todo = {}

    def longest(e):
        if e not in todo:
            whole, widest = sum(d + HOP for _, d in stages[e]), max(d for _, d in stages[e])
            todo[e] = max([longest(s) + (widest if e[0] == s[0] else whole)
                           for s in behind[e]], default=0.0)
        return todo[e]

    for e in reversed(list(after)):
        longest(e)
    clock = dict(pe=0.0, act=0.0, dve=0.0, pool=0.0)
    order = {engine: [] for engine in clock}
    first, taken = {}, {}
    end, can = {}, {e: ARRIVES.get(e[:2], ARRIVES.get(e[0], 0.0)) for e in after}
    holder, bank, table = {}, {}, None
    open_ = [(e, 0) for e in after if not waiting[e]]

    def kind_of(e):
        return e[0], len(stages[e])

    def urgency(e):
        return todo[e] - GROUP_LEAD * group(e) + PRESSING.get(e[0], 0) + PRESSING.get(e[:2], 0)

    def banks(e):
        known = [b for b in range(SHARED) if b not in holder or holder[b] in end]
        return sorted(known, key=lambda b: end[holder[b]] if b in holder else 0.0)[:banks_of(e)]

    def other_table(e):
        want = {"scores": "exp", "gate0": "exp", "gate1": "exp"}.get(e[0], "silu" if e[0] == "up1" else table)
        return want if want != table else None

    while open_:
        starts = []
        for e, s in open_:
            engine = stages[e][s][0]
            if s and first[kind_of(e)][taken.get((kind_of(e), s), 0)] != e:
                continue
            needed = list(frees.get((e, s), ()))
            if e[0] == "stack" and s == 1:
                i = first["stack", 3].index(e)
                needed += [(first["stack", 3][i - 2], 2)] if i >= 2 else []
            fetched = 0.0
            if e[0] == "split" and e[1] >= 2:
                needed += [(("split_low", e[1] - 2, 2), 0)] if e[1] > 2 else [(("split", 0), 0)]
                fetched = end.get(needed[-1], 0.0) + LOAD
            if engine == "pe":
                if len(banks(e)) < banks_of(e):
                    continue
                needed += [holder[b] for b in banks(e) if b in holder]
            if all(k in end for k in needed):
                t = max([clock[engine], can[e], fetched] + [end[k] for k in needed])
                starts.append((t + (TABLE_LOAD if engine == "act" and other_table(e) else 0.0), e, s))
        soonest = min(starts)[0]
        t, e, s = max((x for x in starts if x[0] <= soonest), key=lambda x: urgency(x[1]))
        open_.remove((e, s))
        engine, held = stages[e][s]
        if engine == "act":
            table = other_table(e) or table
        if e[0] in ("gate0", "gate1") and engine == "dve":
            order["act"].append(e)
            clock["act"] = max(clock["act"], t + 1.0)
        if s == 0:
            first.setdefault(kind_of(e), []).append(e)
        else:
            taken[kind_of(e), s] = taken.get((kind_of(e), s), 0) + 1
        if engine == "pe":
            bank[e] = banks(e) or [SHARED + group(e)]
            if banks_of(e):
                for i, b in enumerate(bank[e]):
                    holder[b] = (e, 2 if e[0] == "up1" and i == 0 else reader(e))
        order[engine].append(e)
        clock[engine] = t + held
        end[e, s] = can[e] = t + held + HOP
        last = s + 1 == len(stages[e])
        if not last:
            open_.append((e, s + 1))
        for x in behind[e]:
            if (s == 0) if x[0] == e[0] else last:
                if x[0] != e[0]:
                    can[x] = max(can[x], can[e])
                waiting[x] -= 1
                if not waiting[x]:
                    open_.append((x, 0))
    assert not any(waiting.values())
    return order, max(clock.values()), bank


def order(n):
    return (E1 - 1 + n) % E1


def build(nc, x, ctx, const, weights, qkbias, rows, gates, out):
    orders, _, bank = schedule()
    engines = ("pe", "act", "dve", "pool")
    nth = {}
    for kind in sorted({e[0] for n in engines for e in orders[n]}):
        takes = max(engines, key=lambda n: sum(e[0] == kind for e in orders[n]))
        for i, e in enumerate(e for e in orders[takes] if e[0] == kind):
            nth[e] = i + 1
    low_before, nth_pv_before = {}, {}
    buffer, buffer3 = {}, {}
    for g in range(G):
        scores = [e for e in orders["pe"] if e[0] == "scores" and group(e) == g]
        for i, e in enumerate(scores):
            buffer[e], buffer3[e[1:]] = i % 2, i % NPV
            if i >= 2:
                low = plow(*scores[i - 2][1:])
                low_before[e] = low[0], nth[low]
            if i >= NPV:
                nth_pv_before[e] = nth[("pv",) + scores[i - NPV][1:]]
    nth_split = [1 + 3 * i for i in range(PIECES)]

    def unit(e):
        return CH * e[2] + e[3] if e[0][-1] == "1" else e[2]

    def at_unit(kind, g, k):
        return (kind, g, k, 0) if kind[-1] == "0" else (kind, g, k // CH, k % CH)

    with ExitStack() as stk:
        def sb(name, shape, dt=F32):
            return stk.enter_context(nc.sbuf_tensor(name, shape, dt))

        def sem(name):
            return stk.enter_context(nc.semaphore(name))

        cst = sb("cst", [P, NCONST])
        identb = sb("identb", [P, P], BF16)
        trib = sb("trib", [P, 2, P], BF16)
        headsel = sb("headsel", [P, H, P], BF16)
        pairsel = sb("pairsel", [P, H, SC], BF16)
        neghalf = sb("neghalf", [P, T])
        rowb = sb("rowb", [P, len(ROWS) * P + 8])
        wg = sb("wg", [P, 2, 8])
        wraw = sb("wraw", [P, 2, PIECE])
        wh = sb("wh", [P, sum(USED)], F16)
        wl = sb("wl", [P, sum(USED)], F16)
        X = sb("X", [P, G, T, P])
        cxs = [sb("cxh", [P, B * SC], F16), sb("cxl", [P, B * SC], F16)]
        cxt = [sb("cxth", [P, B, 2, SC], F16), sb("cxtl", [P, B, 2, SC], F16)]
        stat = sb("stat", [P, T, 6])
        mv = sb("mv", [P, 7 * G, T, 2])
        rstd = sb("rstd", [P, 7 * G, T])
        lnx = sb("lnx", [P, G, T, P])
        lni = sb("lni", [P, G, T, P])
        act = sb("act", [P, G, T, P])
        o_n = lnx
        tF = sb("tF", [P, G, GT])
        tH = sb("tH", [P, G, 2, GT], F16)
        tL = sb("tL", [P, G, 2, GT], F16)
        QS = sb("QS", [P, G, QUADS, GT], F16)
        T1 = sb("T1", [P, 2, GT], F16)
        kbs = sb("kbs", [P, 2, QUADS, 4, S], F16)
        KBX = sb("KBX", [P, QUADS, B, 4, SC], F16)
        VBX = [sb("VBXh", [P, 2, B, H // 2, 2 * DV], F16), sb("VBXl", [P, 2, B, H // 2, 2 * DV], F16)]
        VS = [sb("VSh", [P, G, T, H, DV], F16), sb("VSl", [P, G, T, H, DV], F16)]
        MX = sb("MX", [P, B, 2, H])
        MP = sb("MP", [P, B, 2, P], BF16)
        MT = sb("MT", [P, B, S], BF16)
        pr = sb("pr", [P, G, 2, GT])
        prh = sb("prh", [P, G, NPV, GT], F16)
        prl = sb("prl", [P, G, NPV, GT], F16)
        rec = sb("rec", [P, 2, H])
        lg = sb("lg", [P, T, 8])
        zz = sb("zz", [P, T, 8])
        ex = sb("ex", [P, T, 8])
        m8 = sb("m8", [P, T, 8])
        i8 = sb("i8", [P, T, 8], U32)
        i8f = sb("i8f", [P, T, 8])
        sel = sb("sel", [P, 2, T, 8])
        r1 = sb("r1", [P, T, 1])
        r2 = sb("r2", [P, T, 1])
        wt = sb("wt", [P, 2, G, T, 8])
        hr = sb("hr", [P, G, 2, GT])
        KS = [hr[:, g].rearrange("p a k -> p (a k)").bitcast(F16).rearrange("p (j k) -> p j k", j=QUADS) for g in range(G)]
        braw = hr[:, 0]
        bsl = prl[:, 1, 0:2, :]
        ones = prh[:, 1, 0, :]
        cx = lni[:, 0, 0:2, :]
        vtmp = lni[:, 1].rearrange("p t d -> p (t d)")
        hh, hhi, hlo = pr, prh, prl

        ps = [stk.enter_context(nc.psum_tensor(f"ps{i}", [P, GT], F32)) for i in range(8)]

        in_ctx, in_cst, in_x, in_small = sem("in_ctx"), sem("in_cst"), sem("in_x"), sem("in_small")
        in_w, out_done = [sem("in_w0"), sem("in_w1")], sem("out_done")
        zeroed, xb_ready = sem("zeroed"), sem("xb_ready")
        const_ready, bias_rows, bias_ready = sem("const_ready"), sem("bias_rows"), sem("bias_ready")
        ctx_turned, ctx_high, ctx_ready = sem("ctx_turned"), sem("ctx_high"), sem("ctx_ready")
        vctx_mm, vctx_ready = sem("vctx_mm"), sem("vctx_ready")
        w_high, w_ready = sem("w_high"), sem("w_ready")
        stack_mm, stack_high, stack_ready = sem("stack_mm"), sem("stack_high"), sem("stack_ready")
        ln_stat, ln_rstd, ln_done = sem("ln_stat"), sem("ln_rstd"), sem("ln_done")
        turn_mm, turn_first, turn_ready = sem("turn_mm"), sem("turn_first"), sem("turn_ready")
        kb_ready = sem("kb_ready")
        max_mm, max_read, neg_ready = sem("max_mm"), sem("max_read"), sem("neg_ready")
        neg_mm, negT_ready = sem("neg_mm"), sem("negT_ready")
        sc_mm, pr_ready, prh_ready, pv_done = sem("sc_mm"), sem("pr_ready"), sem("prh_ready"), sem("pv_done")
        prl_ready = {"plow": sem("prl_ready"), "plow_pool": sem("prl_ready_pool")}
        o_ready = sem("o_ready")
        sq_mm, sq_read = sem("sq_mm"), sem("sq_read")
        g0_mm, g0_lg, g0_exp, g0_ready = sem("g0_mm"), sem("g0_lg"), sem("g0_exp"), sem("g0_ready")
        g1_mm, g1_lg, g1_sub, g1_exp, g1_ready = sem("g1_mm"), sem("g1_lg"), sem("g1_sub"), sem("g1_exp"), sem("g1_ready")
        up_mm, act_ready, hi_ready, down_mm = (
            [sem(f"{name}{l}") for l in range(2)] for name in ("up_mm", "act_ready", "hi_ready", "down_mm"))
        lo_ready = {kind: sem(f"{kind}_ready") for kind in ("lo0", "lo1", "lo0_dve")}
        hid_ready = [act_ready[0], sem("hid_ready1")]
        down_read, added0 = sem("down_read"), sem("added0")
        add_read = sem("add_read")
        dve_step, act_step, pool_step = sem("dve_step"), sem("act_step"), sem("pool_step")

        ident = cst[:, CONST["ident"]:CONST["ident"] + P]
        sign = {n: cst[:, CONST["signs"] + i:CONST["signs"] + i + 1]
                for i, n in enumerate(["qa", "qb", "ka", "kb", "ba", "bb"])}
        iota = cst[:, CONST["iota"]:CONST["iota"] + 8]

        def row(name):
            i = ROWS.index(name)
            return rowb[:, i * P:(i + 1) * P]

        def rows4(name):
            return row(name).unsqueeze(1).broadcast_to([P, T, P])

        def weight(piece, col):
            o = sum(USED[:piece]) + col
            return wh[:, o:o + P], wl[:, o:o + P]

        LN = {"x0": (X, lnx, 1e-5, None), "x1": (X, lnx, 1e-5, None), "x2": (X, lni, 1e-5, None),
              "a": (act, lnx, 1e-6, ("g1", "b1")), "c": (act, lnx, 1e-6, ("g2", "b2")),
              "f": (act, act, 1e-6, ("g3", "b3")), "x3": (X, lnx, 1e-5, None)}
        TURN = {"x0": (lnx, 0), "o0": (o_n, 1), "x1": (lnx, 0), "x2": (lni, 0), "o1": (o_n, 1),
                "a": (lnx, 0), "o2": (o_n, 1), "c": (lnx, 0), "x3": (lnx, 0)}
        STACK_OF = {"q0": "x0", "q1": "x2", "k1": "x2", "q2": "a"}
        SCALE = [float(D) ** -0.5, float(S) ** -0.5, float(SC) ** -0.5]
        last_unit = {0: 3, 1: 15, 2: 3}

        scaled = [act, lnx]

        def make_low(engine, e):
            g, three, width = group(e), buffer3[e[1:]], GT if e[1] != 1 else S + P
            return engine.tensor_tensor(prl[:, g, three, 0:width], pr[:, g, buffer[("scores",) + e[1:]], 0:width],
                                        prh[:, g, three, 0:width], ALU.subtract)

        def make_hidden_low(engine, e):
            g, k = e[1], unit(e)
            return engine.tensor_tensor(hlo[:, g, k % NPV, :], hh[:, g, k % 2, :], hhi[:, g, k % NPV, :], ALU.subtract)

        block = stk.enter_context(nc.Block())

        @block.sync
        def _(sp):
            def piece(i):
                if i >= 2:
                    sp.wait_ge(w_ready, nth_split[i - 2])
                sp.dma_start(wraw[:, i % 2, 0:USED[i]], weights[:, sum(USED[:i]):sum(USED[:i + 1])]).then_inc(in_w[i % 2], 16)

            sp.dma_start(cx, ctx.rearrange("(t p) d -> p t d", p=P)).then_inc(in_ctx, 16)
            sp.dma_start(cst[:], const).then_inc(in_cst, 16)
            piece(0)
            sp.dma_start(X[:], x.rearrange("(g t p) d -> p g t d", g=G, p=P)).then_inc(in_x, 16)
            sp.wait_ge(zeroed, 1)
            for r in range(2):
                sp.dma_start(braw[r:r + 1, :, :], qkbias).then_inc(bias_rows, 16)
            sp.dma_start(rowb[:], rows.partition_broadcast(P)).then_inc(in_small, 16)
            sp.dma_start(wg[:], gates).then_inc(in_small, 16)
            for i in range(1, PIECES):
                piece(i)
            for g in range(G):
                sp.wait_ge(add_read, nth[("add1", g, E1 - 1)])
                sp.dma_start(out.rearrange("(g t p) d -> p g t d", g=G, p=P)[:, g], X[:, g]).then_inc(out_done, 16)
            sp.wait_ge(out_done, 16 * G)

        @block.gpsimd
        def _(pool):
            step = [0]

            def link(ins):
                step[0] += 1
                ins.then_inc(pool_step, 1)
                pool.wait_ge(pool_step, step[0])

            nc.gpsimd.memset(braw, 0.0).then_inc(zeroed, 1)
            nc.gpsimd.memset(KBX[:].bitcast(U32), 0).then_inc(zeroed, 1)
            nc.gpsimd.memset(neghalf[:], -0.5).then_inc(zeroed, 1)
            for v in VBX:
                nc.gpsimd.memset(v[:], 0.0).then_inc(zeroed, 1)
            nc.gpsimd.memset(MP[:], 0.0).then_inc(zeroed, 1)
            pool.wait_ge(zeroed, 6)
            nc.gpsimd.memset(VBX[0][0:64, :, :, :, D:DV], 1.0).then_inc(zeroed, 1)
            pool.wait_ge(zeroed, 7)
            nc.gpsimd.memset(VBX[0][64:128, :, :, :, D + DV:2 * DV], 1.0).then_inc(zeroed, 1)
            pool.wait_ge(zeroed, 8)
            nc.gpsimd.memset(VS[0][:, :, :, :, D:DV], 1.0).then_inc(zeroed, 1)
            nc.gpsimd.memset(VS[1][:, :, :, :, D:DV], 0.0).then_inc(zeroed, 1)
            for e in orders["pool"]:
                kind, n = e[0], nth[e]
                if kind == "ln_stats":
                    k = n - 1
                    pool.wait_ge(ln_stat, n)
                    link(nc.gpsimd.tensor_scalar(rstd[:, k, :], mv[:, k, :, 1], LN[e[1]][2], None, ALU.add))
                    nc.gpsimd.tensor_tensor(rstd[:, k, :], rstd[:, k, :], neghalf[:], ALU.pow).then_inc(ln_rstd, 1)
                elif kind == "kbs_zero":
                    for i in range(2):
                        nc.gpsimd.memset(kbs[:, i].bitcast(U32), 0).then_inc(zeroed, 1)
                elif kind == "bo_add":
                    pool.wait_ge(in_x, 16)
                    pool.wait_ge(in_small, 32)
                    nc.gpsimd.tensor_tensor(act[:, e[1]], X[:, e[1]], rows4("bo"), ALU.add).then_inc(xb_ready, 1)
                elif kind == "split_low":
                    _, i, j = e
                    pool.wait_ge(w_high, nth[("split", i)])
                    first, end = j * HID, min((j + 1) * HID, USED[i])
                    cols = slice(sum(USED[:i]) + first, sum(USED[:i]) + end)
                    nc.gpsimd.tensor_tensor(wl[:, cols], wraw[:, i % 2, first:end], wh[:, cols],
                                            ALU.subtract).then_inc(w_ready, 1)
                elif kind in ("lo0", "lo1"):
                    l = int(kind[-1])
                    pool.wait_ge(hi_ready[l], nth[(f"hi{l}",) + e[1:]])
                    make_hidden_low(nc.gpsimd, e).then_inc(lo_ready[kind], 1)
                elif kind == "down0":
                    _, g, x_, _ = e
                    pool.wait_ge(down_read, n)
                    if x_ > 0:
                        pool.wait_ge(added0, nth[("down0", g, x_ - 1, 0)])
                    nc.gpsimd.tensor_tensor(X[:, g], X[:, g], scaled[x_ % 2][:, g], ALU.add).then_inc(added0, 1)
                elif kind == "plow_pool":
                    pool.wait_ge(prh_ready, nth[("scores",) + e[1:]])
                    make_low(nc.gpsimd, e).then_inc(prl_ready[kind], 1)

        @block.tensor
        def _(pe):
            emptied = {}
            split_seen = [0]

            def take(b, read_signal, value):
                if b in emptied:
                    pe.wait_ge(*emptied[b])
                emptied[b] = (read_signal, value)

            def need_piece(i):
                if i + 1 > split_seen[0]:
                    pe.wait_ge(w_ready, nth_split[i])
                    split_seen[0] = i + 1

            def split_mm(o, a, b, start=True, stop=True, **kw):
                nc.tensor.matmul(o, a[0], b[0], start=start, stop=False, **kw)
                nc.tensor.matmul(o, a[0], b[1], start=False, stop=False, **kw)
                return nc.tensor.matmul(o, a[1], b[0], start=False, stop=stop, **kw)

            pe.wait_ge(in_cst, 16)
            for e in orders["pe"]:
                kind, n = e[0], nth[e]
                o = ps[bank[e][0]] if e in bank else None
                if kind == "ctx":
                    pe.wait_ge(in_ctx, 16)
                    take(bank[e][0], ctx_ready, 1)
                    for t in range(2):
                        mm = nc.tensor.transpose(o[:, t * P:(t + 1) * P], cx[:, t, :], ident)
                    mm.then_inc(ctx_turned, 1)
                elif kind == "vctx":
                    need_piece(WEIGHTS[f"v{e[1]}"][0])
                    take(bank[e][0], vctx_ready, n)
                    for b in range(B):
                        both = [v[:, b, :, :].rearrange("p a k -> p (a k)") for v in cxt]
                        mm = split_mm(o[:, b * P:(b + 1) * P], both, weight(*WEIGHTS[f"v{e[1]}"]))
                    mm.then_inc(vctx_mm, 1)
                elif kind == "stack":
                    _, name, g, j = e
                    piece, col = WEIGHTS[name]
                    need_piece(piece)
                    if name in ("k0", "k2"):
                        src, width = [v[:] for v in cxs], B * SC
                        if n == 1:
                            pe.wait_ge(ctx_ready, 3)
                    else:
                        src, width = [tH[:, g, 0, :], tL[:, g, 0, :]], GT
                        if j == 0:
                            pe.wait_ge(turn_ready, nth[("turn", STACK_OF[name], g)])
                    take(bank[e][0], stack_ready, n)
                    biased = name in ("q0", "k0")
                    mm = split_mm(o[:, 0:width], weight(piece, col + j * P), src, stop=not biased)
                    if biased:
                        if n == 1:
                            pe.wait_ge(bias_ready, 1)
                            pe.wait_ge(const_ready, 2)
                        mm = nc.tensor.matmul(o[:, 0:width], bsl[:, 0 if name == "q0" else 1, j * P:(j + 1) * P],
                                              ones[:, 0:width], start=False, stop=True)
                    mm.then_inc(stack_mm, 1)
                elif kind == "turn":
                    _, name, g = e
                    src = TURN[name][0]
                    if name[:1] == "o":
                        pe.wait_ge(o_ready, nth[("out_norm", int(name[1]), 2 * g + 1)])
                    else:
                        pe.wait_ge(ln_done, nth[("ln_norm", name, g)])
                    take(bank[e][0], turn_ready, n)
                    for t in range(T):
                        mm = nc.tensor.transpose(o[:, t * P:(t + 1) * P], src[:, g, t, :], ident)
                    mm.then_inc(turn_mm, 1)
                elif kind == "square":
                    _, name, g = e
                    slot = 1 if name[:1] == "o" else 0
                    need_piece(WEIGHTS[name][0])
                    pe.wait_ge(turn_ready, nth[("turn", {"v1": "x2", "f": "c"}.get(name, name), g)])
                    take(bank[e][0], sq_read, n)
                    for t in range(T):
                        tt = slice(t * P, (t + 1) * P)
                        mm = split_mm(o[:, tt], (tH[:, g, slot, tt], tL[:, g, slot, tt]), weight(*WEIGHTS[name]))
                    mm.then_inc(sq_mm, 1)
                elif kind == "max":
                    _, a, b, u = e
                    g = b // 2
                    take(bank[e][0], max_read, n)
                    q0 = (b % 2) * S
                    if a != 1:
                        if u == 0:
                            pe.wait_ge(stack_ready, nth[("stack", f"q{a}", g, QUADS - 1)])
                            pe.wait_ge(stack_ready, nth[("stack", f"k{a}", 0, QUADS - 1)])
                        qt, half = u // 2, u % 2
                        for i in range(2):
                            j = 2 * half + i
                            mm = nc.tensor.matmul(o[:, i * S:(i + 1) * S], QS[:, g, j, q0 + qt * P:q0 + (qt + 1) * P],
                                                  KBX[:, j, b, :, :].rearrange("p h k -> p (h k)"), start=True, stop=True)
                    else:
                        if u == 0:
                            pe.wait_ge(kb_ready, nth[("kblocks", 1, b)])
                            pe.wait_ge(const_ready, 5)
                            pe.wait_ge(stack_ready, nth[("stack", "q1", g, QUADS - 1)])
                        kb = kbs[:, b % 2]
                        if u < 4:
                            v, heads = o[:].rearrange("p (h k) -> p h k", h=4), 4
                            nc.tensor.matmul(v, QS[:, g, u, q0:q0 + P], kb[:, u, :, 0:P], start=True, stop=True)
                        else:
                            j, h0 = (u - 4) // 2, 2 * ((u - 4) % 2)
                            v, heads = o[:].rearrange("p (h k) -> p h k", h=2), 2
                            nc.tensor.matmul(v, QS[:, g, j, q0 + P:q0 + 2 * P], kb[:, j, h0:h0 + 2, :], start=True,
                                             stop=True)
                            v = v[:, :, P:2 * P]
                        mm = nc.tensor.matmul(v, identb[:], trib[:, 0, :].unsqueeze(1).broadcast_to([P, heads, P]),
                                              start=False, stop=True, skip_group_check=True)
                    mm.then_inc(max_mm, 1)
                elif kind == "negmax":
                    pe.wait_ge(neg_ready, n)
                    take(bank[e][0], negT_ready, n)
                    for t in range(2):
                        mm = nc.tensor.matmul(o[:, t * P:(t + 1) * P], MP[:, e[2], t, :], identb[:], start=True, stop=True)
                    mm.then_inc(neg_mm, 1)
                elif kind == "scores":
                    _, a, b, u = e
                    g = b // 2
                    if u == 0:
                        pe.wait_ge(negT_ready, nth[("negmax", a, b)])
                        pe.wait_ge(const_ready, 5 if a == 1 else 3)
                    take(bank[e][0], prh_ready, n)
                    q0 = (b % 2) * S
                    mt = MT[:, b, :]
                    if a != 1:
                        for i in range(2):
                            p = 2 * u + i
                            nc.tensor.matmul(o[:, i * S:(i + 1) * S],
                                             KBX[:, p // 2, b, 2 * (p % 2):2 * (p % 2) + 2, :].rearrange("p h k -> p (h k)"),
                                             QS[:, g, p // 2, q0:q0 + S], start=True, stop=False)
                            mm = nc.tensor.matmul(o[:, i * S:(i + 1) * S],
                                                  pairsel[:, 2 * p:2 * p + 2, :].rearrange("p h k -> p (h k)"), mt,
                                                  start=False, stop=True)
                    else:
                        kb = kbs[:, b % 2]
                        j, h = u // 4, u % 4
                        kw = dict(start=False, stop=True, skip_group_check=True)
                        nc.tensor.matmul(o[:, 0:S], kb[:, j, h, 0:P], QS[:, g, j, q0:q0 + S], start=True, stop=True)
                        nc.tensor.matmul(o[:, S:S + P], kb[:, j, h, P:2 * P], QS[:, g, j, q0 + P:q0 + S], **kw)
                        nc.tensor.matmul(o[:, 0:S], headsel[:, u, :], mt, **kw)
                        nc.tensor.matmul(o[:, S:S + P], headsel[:, u, :], mt[:, P:S], **kw)
                        for c in (0, S):
                            mm = nc.tensor.matmul(o[:, c:c + P], identb[:], trib[:, 1, :], **kw)
                    mm.then_inc(sc_mm, 1)
                elif kind == "pv":
                    _, a, b, u = e
                    g = b // 2
                    low = plow(a, b, u)
                    pe.wait_ge(prl_ready[low[0]], nth[low])
                    if u == 0:
                        take(bank[e][0], o_ready, nth[("out_norm", a, b)])
                        if a == 1:
                            pe.wait_ge(sq_read, nth[("square", "v1", g)])
                        else:
                            pe.wait_ge(vctx_ready, a // 2 + 1)
                    ph, pl = prh[:, g, buffer3[e[1:]], :], prl[:, g, buffer3[e[1:]], :]
                    if a != 1:
                        for i in range(2):
                            p = 2 * u + i
                            for qt in range(2):
                                c = qt * H * DV + p * 2 * DV
                                cc = slice(i * S + qt * P, i * S + (qt + 1) * P)
                                mm = split_mm(o[:, c:c + 2 * DV], (ph[:, cc], pl[:, cc]),
                                              [v[:, a // 2, b, p, :] for v in VBX])
                    else:
                        t0 = 2 * (b % 2)
                        c = u * DV
                        v0 = [v[:, g, t0, u, :] for v in VS]
                        v1 = [v[:, g, t0 + 1, u, :] for v in VS]
                        split_mm(o[:, c:c + DV], (ph[:, 0:P], pl[:, 0:P]), v0)
                        c += H * DV
                        split_mm(o[:, c:c + DV], (ph[:, P:2 * P], pl[:, P:2 * P]), v0, stop=False)
                        mm = split_mm(o[:, c:c + DV], (ph[:, S:S + P], pl[:, S:S + P]), v1, start=False)
                    mm.then_inc(pv_done, 1)
                elif kind in ("gate0", "gate1"):
                    g = e[1]
                    l = 0 if kind == "gate0" else 1
                    pe.wait_ge(in_small, 32)
                    pe.wait_ge(turn_first, nth[("turn", "x1" if l == 0 else "x3", g)])
                    take(bank[e][0], (g0_lg, g1_lg)[l], n)
                    for t in range(T):
                        mm = nc.tensor.matmul(o[:, t * 8:(t + 1) * 8], tF[:, g, t * P:(t + 1) * P], wg[:, l, :],
                                              start=True, stop=True)
                    mm.then_inc((g0_mm, g1_mm)[l], 1)
                elif kind in ("up0", "up1"):
                    _, g, x_, c = e
                    l = int(kind[-1])
                    tt = (tH[:, g, 0, :], tL[:, g, 0, :])
                    pe.wait_ge(turn_ready, nth[("turn", "x1" if l == 0 else "x3", g)])
                    if l == 0:
                        need_piece(2)
                        take(bank[e][0], act_ready[0], n)
                        mm = split_mm(o[:], weight(1, x_ * P), tt)
                    else:
                        need_piece(FIRST1 + x_)
                        take(bank[e][0], hid_ready[1], n)
                        take(bank[e][1], act_ready[1], n)
                        split_mm(o[:], weight(FIRST1 + x_, c * P), tt)
                        mm = split_mm(ps[bank[e][1]][:], weight(FIRST1 + x_, HID + c * P), tt)
                    mm.then_inc(up_mm[l], 1)
                elif kind in ("down0", "down1"):
                    _, g, x_, c = e
                    l, k = int(kind[-1]), unit(e)
                    low = low_step(l, *e[1:])
                    pe.wait_ge(lo_ready[low[0]], nth[low])
                    if l == 0:
                        take(bank[e][0], down_read, n)
                        w = weight(2, x_ * P)
                    else:
                        if c == 0:
                            take(bank[e][0], add_read, nth[("add1", g, x_)])
                        w = weight(FIRST1 + x_, 2 * HID + c * P)
                    for t in range(T):
                        tt = slice(t * P, (t + 1) * P)
                        hparts = (hhi[:, g, k % NPV, tt], hlo[:, g, k % NPV, tt])
                        if l == 0:
                            mm = split_mm(o[:, tt], hparts, w)
                        else:
                            mm = split_mm(o[:, tt], hparts, w, start=(c == 0 and t == 0), stop=(c == CH - 1),
                                          skip_group_check=True)
                    mm.then_inc(down_mm[l], 1)

        @block.scalar
        def _(sc):
            step = [0]
            for e in orders["act"]:
                kind, n = e[0], nth[e]
                src = ps[bank[e][0]] if e in bank else None
                if kind == "ctx":
                    sc.wait_ge(ctx_turned, 1)
                    nc.scalar.copy(cxs[0][:], src[:, 0:B * SC]).then_inc(ctx_high, 1)
                elif kind == "stack":
                    _, name, g, j = e
                    width = B * SC if name in ("k0", "k2") else GT
                    sc.wait_ge(stack_mm, n)
                    if n > 2:
                        sc.wait_ge(stack_ready, n - 2)
                    nc.scalar.activation(T1[:, n % 2, 0:width], src[:, 0:width], ACT.Copy,
                                         scale=sign[name[0] + "b"]).then_inc(stack_high, 1)
                elif kind == "turn":
                    _, name, g = e
                    sc.wait_ge(turn_mm, n)
                    dst = tF[:, g, :] if name in ("x1", "x3") else tH[:, g, TURN[name][1], :]
                    nc.scalar.copy(dst, src[:]).then_inc(turn_first, 1)
                elif kind == "negmax":
                    sc.wait_ge(neg_mm, n)
                    nc.scalar.copy(MT[:, e[2], :], src[:, 0:S]).then_inc(negT_ready, 1)
                elif kind == "scores":
                    _, a, b, u = e
                    g = b // 2
                    sc.wait_ge(sc_mm, n)
                    if e in low_before:
                        kind_before, nth_before = low_before[e]
                        sc.wait_ge(prl_ready[kind_before], nth_before)
                    width = GT if a != 1 else S + P
                    nc.scalar.activation(pr[:, g, buffer[e], 0:width], src[:, 0:width], ACT.Exp,
                                         scale=SCALE[a]).then_inc(pr_ready, 1)
                    if e in nth_pv_before:
                        sc.wait_ge(pv_done, nth_pv_before[e])
                    nc.scalar.activation(prh[:, g, buffer3[e[1:]], 0:width], src[:, 0:width], ACT.Exp,
                                         scale=SCALE[a]).then_inc(prh_ready, 1)
                elif kind == "gate0":
                    sc.wait_ge(g0_lg, n)
                    nc.scalar.activation(ex[:], lg[:], ACT.Exp, scale=-1.0).then_inc(g0_exp, 1)
                elif kind == "gate1":
                    sc.wait_ge(g1_sub, n)
                    nc.scalar.activation(ex[:], zz[:], ACT.Exp).then_inc(g1_exp, 1)
                elif kind == "up0":
                    g, k = e[1], unit(e)
                    sc.wait_ge(up_mm[0], n)
                    if k >= 2:
                        sc.wait_ge(act_ready[0], nth[(kind, g, k - 2, 0)])
                        low = low_step(0, g, k - 2, 0)
                        sc.wait_ge(lo_ready[low[0]], nth[low])
                    step[0] += 1
                    nc.scalar.activation(hr[:, g, k % 2, :], src[:], ACT.Relu).then_inc(act_step, 1)
                    sc.wait_ge(act_step, step[0])
                    nc.scalar.activation(hh[:, g, k % 2, :], hr[:, g, k % 2, :], ACT.Square).then_inc(act_ready[0], 1)
                elif kind == "up1":
                    g, k = e[1], unit(e)
                    sc.wait_ge(up_mm[1], n)
                    if k >= 2:
                        sc.wait_ge(hid_ready[1], nth[at_unit(kind, g, k - 2)])
                    nc.scalar.activation(hr[:, g, k % 2, :], ps[bank[e][1]][:], ACT.Silu).then_inc(act_ready[1], 1)
                elif kind in ("hi0", "hi1"):
                    l, k, g = int(kind[-1]), unit(e), e[1]
                    sc.wait_ge(hid_ready[l], nth[(f"up{l}",) + e[1:]])
                    if k >= NPV:
                        sc.wait_ge(down_mm[l], nth[at_unit(f"down{l}", g, k - NPV)])
                    nc.scalar.copy(hhi[:, g, k % NPV, :], hh[:, g, k % 2, :]).then_inc(hi_ready[l], 1)
                elif kind == "down0":
                    _, g, x_, _ = e
                    sc.wait_ge(down_mm[0], n)
                    if x_ >= 2:
                        sc.wait_ge(added0, nth[("down0", g, x_ - 2, 0)])
                    y, dst = src[:].rearrange("p (t d) -> p t d", t=T), scaled[x_ % 2]
                    if x_ == E0 - 1:
                        ins = nc.scalar.copy(dst[:, g], y)
                    else:
                        sc.wait_ge(g0_ready, nth[("gate0", g)])
                        for t in range(T):
                            ins = nc.scalar.activation(dst[:, g, t, :], y[:, t, :], ACT.Copy,
                                                       scale=wt[:, 0, g, t, x_:x_ + 1])
                    ins.then_inc(down_read, 1)

        @block.vector
        def _(dve):
            step = [0]

            def link(ins):
                step[0] += 1
                ins.then_inc(dve_step, 1)
                dve.wait_ge(dve_step, step[0])

            dve.wait_ge(in_cst, 16)
            nc.vector.tensor_copy(identb[:], ident).then_inc(const_ready, 1)
            nc.vector.memset(ones, 1.0).then_inc(const_ready, 1)
            for e in orders["dve"]:
                kind, n = e[0], nth[e]
                src = ps[bank[e][0]] if e in bank else None
                if kind == "bias":
                    dve.wait_ge(bias_rows, 32)
                    hi = T1[:]
                    link(nc.vector.tensor_scalar(hi, braw, sign["bb"], None, ALU.mult))
                    nc.vector.scalar_tensor_tensor(bsl, braw, sign["ba"], hi, ALU.mult,
                                                   ALU.add).then_inc(bias_ready, 1)
                elif kind == "masks0":
                    heads = cst[:, CONST["heads"]:CONST["heads"] + H].unsqueeze(2)
                    nc.vector.tensor_copy(pairsel[:], heads.broadcast_to([P, H, SC])).then_inc(const_ready, 1)
                elif kind == "masks1":
                    nc.vector.tensor_copy(trib[:].rearrange("p a k -> p (a k)"),
                                          cst[:, CONST["tri_q"]:CONST["tri_q"] + 2 * P]).then_inc(const_ready, 1)
                    heads = cst[:, CONST["heads"]:CONST["heads"] + H].unsqueeze(2)
                    nc.vector.tensor_copy(headsel[:], heads.broadcast_to([P, H, P])).then_inc(const_ready, 1)
                elif kind == "split":
                    i = e[1]
                    cols = slice(sum(USED[:i]), sum(USED[:i + 1]))
                    raw, hi, lo = wraw[:, i % 2, 0:USED[i]], wh[:, cols], wl[:, cols]
                    dve.wait_ge(in_w[i % 2], 16 * (i // 2 + 1))
                    nc.vector.tensor_copy(hi, raw).then_inc(w_high, 1)
                    if i == 0:
                        dve.wait_ge(w_high, 1)
                        nc.vector.tensor_tensor(lo, raw, hi, ALU.subtract).then_inc(w_ready, 1)
                elif kind == "ctx":
                    dve.wait_ge(ctx_high, 1)
                    nc.vector.tensor_tensor(cxs[1][:], src[:, 0:B * SC], cxs[0][:], ALU.subtract).then_inc(ctx_ready, 1)
                    dve.wait_ge(ctx_ready, 1)
                    for i in range(2):
                        nc.vector.tensor_copy(cxt[i][:], cxs[i][:].rearrange("p (b k) -> p b k", b=B).unsqueeze(2)
                                              .broadcast_to([P, B, 2, SC])).then_inc(ctx_ready, 1)
                elif kind == "vctx":
                    dve.wait_ge(vctx_mm, n)
                    dve.wait_ge(zeroed, 10)
                    dve.wait_ge(in_small, 32)
                    if e[1] == 0:
                        link(nc.vector.tensor_tensor(vtmp.rearrange("p (b d) -> p b d", b=B),
                                                     src[:].rearrange("p (b d) -> p b d", b=B),
                                                     row("bv").unsqueeze(1).broadcast_to([P, B, P]), ALU.add))
                    else:
                        link(nc.vector.tensor_copy(vtmp, src[:]))
                    for half in range(2):
                        pp = slice(64 * half, 64 * half + 64)
                        v = vtmp[pp, :].rearrange("p (be two d) -> p be two d", two=2, d=D)[:, :, half, :]
                        dst = [t[pp, e[1] // 2].rearrange("p b e (two d) -> p (b e) two d", two=2)[:, :, half, 0:D] for t in VBX]
                        link(nc.vector.tensor_copy(dst[0], v))
                        ins = nc.vector.tensor_tensor(dst[1], v, dst[0], ALU.subtract)
                    ins.then_inc(vctx_ready, 1)
                elif kind == "stack":
                    _, name, g, j = e
                    width = B * SC if name in ("k0", "k2") else GT
                    dve.wait_ge(stack_high, n)
                    t1 = T1[:, n % 2, :]
                    sa = sign[name[0] + "a"]
                    if name in ("k0", "k2"):
                        dve.wait_ge(zeroed, 2)
                        for h in range(4):
                            pp = slice(SLOT * h, SLOT * (h + 1))
                            ins = nc.vector.scalar_tensor_tensor(
                                KBX[pp, j, :, h, :], src[pp, 0:width].rearrange("p (b k) -> p b k", b=B), sa[pp, :],
                                t1[pp, 0:width].rearrange("p (b k) -> p b k", b=B), ALU.mult, ALU.add)
                    else:
                        dst = QS[:, g, j, :] if name[:1] == "q" else KS[g][:, j, :]
                        ins = nc.vector.scalar_tensor_tensor(dst, src[:], sa, t1, ALU.mult, ALU.add)
                    ins.then_inc(stack_ready, 1)
                elif kind == "turn":
                    _, name, g = e
                    slot = TURN[name][1]
                    dve.wait_ge(turn_first, n)
                    whole = src[:]
                    if name in ("x1", "x3"):
                        whole = tF[:, g, :]
                        link(nc.vector.tensor_copy(tH[:, g, slot, :], whole))
                    nc.vector.tensor_tensor(tL[:, g, slot, :], whole, tH[:, g, slot, :], ALU.subtract).then_inc(turn_ready, 1)
                elif kind == "kblocks":
                    b = e[2]
                    dve.wait_ge(zeroed, 12)
                    dve.wait_ge(stack_ready, nth[("stack", "k1", b // 2, QUADS - 1)])
                    if b >= 2:
                        dve.wait_ge(sc_mm, nth[("scores", 1, b - 2, 15)])
                    for h in range(4):
                        pp = slice(SLOT * h, SLOT * (h + 1))
                        ins = nc.vector.tensor_copy(kbs[pp, b % 2, :, h, :], KS[b // 2][pp, :, (b % 2) * S:(b % 2) * S + S])
                    ins.then_inc(kb_ready, 1)
                elif kind == "ln_stats":
                    _, name, g = e
                    from_ = LN[name][0]
                    if name == "x0":
                        dve.wait_ge(in_x, 16)
                    if name == "x2":
                        dve.wait_ge(added0, nth[("down0", g, E0 - 1, 0)])
                    if n > 1:
                        dve.wait_ge(ln_stat, n - 1)
                    for t in range(T):
                        ins = nc.vector.bn_stats(stat[:, t, :], from_[:, g, t, :])
                    link(ins)
                    for t in range(T):
                        ins = nc.vector.bn_aggr(mv[:, n - 1, t, :], stat[:, t, :])
                    ins.then_inc(ln_stat, 1)
                elif kind == "ln_norm":
                    _, name, g = e
                    from_, dst, _, affine = LN[name]
                    k = nth[("ln_stats", name, g)] - 1
                    dve.wait_ge(ln_rstd, k + 1)
                    for t in range(T):
                        ins = nc.vector.tensor_scalar(dst[:, g, t, :], from_[:, g, t, :], mv[:, k, t, 0:1], rstd[:, k, t:t + 1],
                                                      ALU.subtract, ALU.mult)
                    if affine:
                        link(ins)
                        link(nc.vector.tensor_tensor(dst[:, g], dst[:, g], rows4(affine[0]), ALU.mult))
                        ins = nc.vector.tensor_tensor(dst[:, g], dst[:, g], rows4(affine[1]), ALU.add)
                    if name == "f":
                        link(ins)
                        ins = nc.vector.tensor_tensor(X[:, g], X[:, g], act[:, g], ALU.add)
                    ins.then_inc(ln_done, 1)
                    dve.wait_ge(ln_done, n)
                elif kind == "max":
                    _, a, b, u = e
                    dve.wait_ge(max_mm, n)
                    if a != 1:
                        o, heads = MX[:, b, u // 2, 8 * (u % 2):8 * (u % 2) + 8], 8
                    elif u < 4:
                        o, heads = MX[:, b, 0, 4 * u:4 * u + 4], 4
                    else:
                        o, heads = MX[:, b, 1, 2 * (u - 4):2 * (u - 4) + 2], 2
                    nc.vector.tensor_reduce(o, src[:].rearrange("p (h k) -> p h k", h=heads), AX_X,
                                            ALU.max).then_inc(max_read, 1)
                elif kind == "negmax":
                    _, a, b = e
                    dve.wait_ge(max_read, nth[("max", a, b, 11 if a == 1 else 3)])
                    dve.wait_ge(zeroed, 10)
                    link(nc.vector.tensor_scalar(MP[:, b, :, 0:H], MX[:, b], -1.0, None, ALU.mult))
                    nc.vector.scalar_tensor_tensor(MP[:, b, :, H:2 * H], MX[:, b], -1.0, MP[:, b, :, 0:H], ALU.mult,
                                                   ALU.subtract).then_inc(neg_ready, 1)
                elif kind == "plow":
                    dve.wait_ge(prh_ready, nth[("scores",) + e[1:]])
                    make_low(nc.vector, e).then_inc(prl_ready[kind], 1)
                elif kind == "out_norm":
                    _, a, b = e
                    g = b // 2
                    dve.wait_ge(pv_done, nth[("pv", a, b, last_unit[a])])
                    v = ps[SHARED + g][:, 0:2 * H * DV].rearrange("p (q h d) -> p q h d", q=2, d=DV)
                    if n > 1:
                        dve.wait_ge(o_ready, n - 1)
                    link(nc.vector.reciprocal(rec[:], v[:, :, :, D]))
                    for q in range(2):
                        ins = nc.vector.tensor_tensor(
                            o_n[:, g, 2 * (b % 2) + q, :].rearrange("p (h d) -> p h d", d=D), v[:, q, :, 0:D],
                            rec[:, q, :].unsqueeze(2).broadcast_to([P, H, D]), ALU.mult)
                    ins.then_inc(o_ready, 1)
                elif kind == "square":
                    _, name, g = e
                    dve.wait_ge(sq_mm, n)
                    y = src[:].rearrange("p (t d) -> p t d", t=T)
                    if name == "o0":
                        dve.wait_ge(xb_ready, nth[("bo_add", g)])
                        ins = nc.vector.tensor_tensor(X[:, g], y, act[:, g], ALU.add)
                    elif name == "v1":
                        v = src[:].rearrange("p (t h d) -> p t h d", t=T, d=D)
                        link(nc.vector.tensor_copy(VS[0][:, g, :, :, 0:D], v))
                        ins = nc.vector.tensor_tensor(VS[1][:, g, :, :, 0:D], v, VS[0][:, g, :, :, 0:D], ALU.subtract)
                    elif name == "o1":
                        link(nc.vector.tensor_tensor(act[:, g], y, rows4("bo1"), ALU.add))
                        ins = nc.vector.scalar_tensor_tensor(act[:, g], act[:, g], 0.0, lni[:, g], ALU.max, ALU.add)
                    elif name == "o2":
                        link(nc.vector.tensor_tensor(act[:, g], y, rows4("bo2"), ALU.add))
                        ins = nc.vector.tensor_scalar(act[:, g], act[:, g], 0.0, 2.0, ALU.max, ALU.mult)
                    else:
                        link(nc.vector.tensor_tensor(act[:, g], y, rows4("bf"), ALU.add))
                        ins = nc.vector.scalar_tensor_tensor(act[:, g], act[:, g], 0.0, lnx[:, g], ALU.max, ALU.add)
                    ins.then_inc(sq_read, 1)
                    dve.wait_ge(sq_read, n)
                elif kind == "gate0":
                    g = e[1]
                    dve.wait_ge(g0_mm, n)
                    nc.vector.tensor_copy(lg[:].rearrange("p t x -> p (t x)"), src[:, 0:8 * T]).then_inc(g0_lg, 1)
                    dve.wait_ge(g0_lg, n)
                    lb = rowb[:, len(ROWS) * P:len(ROWS) * P + 8]
                    link(nc.vector.tensor_tensor(zz[:], lg[:], lb.unsqueeze(1).broadcast_to([P, T, 8]), ALU.add))
                    for t in range(T):
                        ins = nc.vector.max(m8[:, t, :], zz[:, t, :])
                    link(ins)
                    for t in range(T):
                        ins = nc.vector.max_index(i8[:, t, :], m8[:, t, :], zz[:, t, :])
                    link(ins)
                    link(nc.vector.tensor_copy(i8f[:], i8[:]))
                    for k in range(2):
                        ins = nc.vector.tensor_tensor(sel[:, k], iota.unsqueeze(1).broadcast_to([P, T, 8]),
                                                      i8f[:, :, k:k + 1].broadcast_to([P, T, 8]), ALU.is_equal)
                    link(ins)
                    link(nc.vector.tensor_tensor(sel[:, 0], sel[:, 0], sel[:, 1], ALU.add))
                    dve.wait_ge(g0_exp, n)
                    link(nc.vector.tensor_scalar(zz[:], ex[:], 1.0, None, ALU.add))
                    link(nc.vector.reciprocal(zz[:], zz[:]))
                    link(nc.vector.tensor_tensor(zz[:], zz[:], sel[:, 0], ALU.mult))
                    link(nc.vector.tensor_reduce(r1[:], zz[:], AX_X, ALU.add))
                    link(nc.vector.tensor_scalar(r1[:], r1[:], 1e-6, None, ALU.add))
                    link(nc.vector.reciprocal(r2[:], r1[:]))
                    nc.vector.tensor_tensor(wt[:, 0, g], zz[:], r2[:].broadcast_to([P, T, 8]), ALU.mult).then_inc(g0_ready, 1)
                    dve.wait_ge(g0_ready, n)
                elif kind == "gate1":
                    g = e[1]
                    dve.wait_ge(g1_mm, n)
                    nc.vector.tensor_copy(lg[:].rearrange("p t x -> p (t x)"), src[:, 0:8 * T]).then_inc(g1_lg, 1)
                    dve.wait_ge(g1_lg, n)
                    link(nc.vector.tensor_reduce(r1[:], lg[:], AX_X, ALU.max))
                    nc.vector.tensor_tensor(zz[:], lg[:], r1[:].broadcast_to([P, T, 8]), ALU.subtract).then_inc(g1_sub, 1)
                    dve.wait_ge(g1_exp, n)
                    link(nc.vector.tensor_reduce(r1[:], ex[:], AX_X, ALU.add))
                    link(nc.vector.reciprocal(r2[:], r1[:]))
                    link(nc.vector.tensor_tensor(zz[:], ex[:], r2[:].broadcast_to([P, T, 8]), ALU.mult))
                    for t in range(T):
                        ins = nc.vector.max(m8[:, t, :], zz[:, t, :])
                    link(ins)
                    for t in range(T):
                        ins = nc.vector.max_index(i8[:, t, :], m8[:, t, :], zz[:, t, :])
                    link(ins)
                    link(nc.vector.tensor_copy(i8f[:], i8[:]))
                    link(nc.vector.tensor_tensor(sel[:, 0], iota.unsqueeze(1).broadcast_to([P, T, 8]),
                                                 i8f[:, :, 0:1].broadcast_to([P, T, 8]), ALU.is_equal))
                    link(nc.vector.tensor_tensor(sel[:, 0], sel[:, 0], m8[:, :, 0:1].broadcast_to([P, T, 8]), ALU.mult))
                    nc.vector.tensor_scalar(wt[:, 1, g], sel[:, 0], 2.0, None, ALU.mult).then_inc(g1_ready, 1)
                    dve.wait_ge(g1_ready, n)
                elif kind == "lo0_dve":
                    dve.wait_ge(hi_ready[0], nth[("hi0",) + e[1:]])
                    make_hidden_low(nc.vector, e).then_inc(lo_ready[kind], 1)
                elif kind == "up1":
                    g, k = e[1], unit(e)
                    dve.wait_ge(act_ready[1], n)
                    if k >= 2:
                        dve.wait_ge(lo_ready["lo1"], nth[at_unit("lo1", g, k - 2)])
                    nc.vector.tensor_tensor(hh[:, g, k % 2, :], src[:], hr[:, g, k % 2, :], ALU.mult).then_inc(hid_ready[1], 1)
                elif kind == "add1":
                    _, g, x_ = e
                    dve.wait_ge(down_mm[1], nth[("down1", g, x_, CH - 1)])
                    if x_ > 0:
                        dve.wait_ge(add_read, nth[("add1", g, x_ - 1)])
                    y = ps[SHARED + g][:].rearrange("p (t d) -> p t d", t=T)
                    if x_ == 0:
                        ins = nc.vector.tensor_tensor(X[:, g], y, X[:, g], ALU.add)
                    else:
                        k = order(x_)
                        for t in range(T):
                            ins = nc.vector.scalar_tensor_tensor(X[:, g, t, :], y[:, t, :], wt[:, 1, g, t, k:k + 1],
                                                                 X[:, g, t, :], ALU.mult, ALU.add)
                    ins.then_inc(add_read, 1)


def _pack(inputs):
    f = {k: np.ascontiguousarray(v) for k, v in inputs.items()}

    def stack(w):
        w = w.reshape(w.shape[0], QUADS, 4, 1, D)
        w = np.concatenate([w, w, w, np.zeros_like(w)], axis=3)
        return w.reshape(w.shape[0], QUADS * P)

    def per_head(w):
        return w.transpose(1, 0, 2).reshape(P, P)

    const = np.zeros((P, NCONST), np.float32)
    const[:, 0:P] = np.eye(P)
    q, k = np.meshgrid(np.arange(P), np.arange(P), indexing="ij")
    const[:, P:2 * P] = np.where(k > q, NEG, 0.0)
    const[:, 2 * P:3 * P] = np.where(q > k, NEG, 0.0)
    third = (np.arange(P) % SLOT) // D
    for i, low in ((0, 2), (2, 1)):
        const[:, 384 + i] = third == low
        const[:, 385 + i] = np.where(third == low, -1.0, 1.0)
    const[:, 388] = np.arange(P) == 1
    const[:, 389] = np.where(np.arange(P) == 1, -1.0, 1.0)
    const[:, 390:398] = np.arange(8)
    const[:, 398:414] = (np.arange(P)[:, None] % H == np.arange(H)) & (np.arange(P)[:, None] < 2 * H)
    Wk, Wq = [f["L0_xattn_Wk"].T, per_head(f["L1_xattn_Wk1"]), per_head(f["L1_xattn_Wk2"])], [
        f["L0_xattn_Wq"].T, per_head(f["L1_xattn_Wq1"]), per_head(f["L1_xattn_Wq2"])]
    Wv = [f["L0_xattn_Wv"].T, per_head(f["L1_xattn_Wv1"]), per_head(f["L1_xattn_Wv2"])]
    Wo = [f["L0_xattn_Wo"].T, f["L1_xattn_Wo1"], f["L1_xattn_Wo2"]]
    weights = []
    for i in range(3):
        parts = [stack(Wk[i]), stack(Wq[i]), Wv[i], Wo[i]] + ([f["L1_xattn_Wf"]] if i == 2 else [])
        weights.append(np.concatenate(parts, axis=1))
    rows = np.concatenate([f[n] for n in (
        "L0_xattn_bv", "L0_xattn_bo", "L1_xattn_bo1", "L1_xattn_g1", "L1_xattn_b1", "L1_xattn_bo2", "L1_xattn_g2",
        "L1_xattn_b2", "L1_xattn_bf", "L1_xattn_g3", "L1_xattn_b3", "L0_ffn_lb_bias")])
    weights[1:1] = [
        np.concatenate([f["L0_ffn_w1"].transpose(2, 0, 1).reshape(P, -1), f["L0_ffn_cfc"].T], axis=1),
        np.concatenate([f["L0_ffn_w2"].transpose(2, 0, 1).reshape(P, -1), f["L0_ffn_cproj"].T], axis=1)]

    def down(w):
        return w.reshape(-1, CH, P, P).transpose(2, 0, 1, 3).reshape(P, -1, HID)

    w1 = np.concatenate([
        np.concatenate([f["L1_ffn_w_up"], f["L1_ffn_ws_up"][None]]).transpose(1, 0, 2),
        np.concatenate([f["L1_ffn_w_gate"], f["L1_ffn_ws_gate"][None]]).transpose(1, 0, 2),
        down(np.concatenate([f["L1_ffn_w_down"], f["L1_ffn_ws_down"][None]]))], axis=2)
    for n in range(E1):
        weights.append(w1[:, order(n)])
    return {
        "x": f["x"].reshape(-1, P), "ctx": f["ctx_1024"].reshape(-1, P), "const": const,
        "weights": np.concatenate(weights, axis=1),
        "qkbias": np.stack([stack(f["L0_xattn_bq"][None])[0], stack(f["L0_xattn_bk"][None])[0]])[None], "rows": rows,
        "gates": np.stack([f["L0_ffn_gate_w"].T, f["L1_ffn_w_router"]], axis=1),
    }


def kernel(**inputs):
    import concourse.bacc as _bacc
    from concourse.bass_utils import run_bass_kernel_spmd as _run

    nc = _bacc.Bacc("TRN2", target_bir_lowering=False, num_devices=1)
    arrays, args = {}, []
    for name, a in _pack({k: np.asarray(v) for k, v in inputs.items()}).items():
        a = np.ascontiguousarray(a)
        arrays[f"in_{name}"] = a
        args.append(nc.dram_tensor(f"in_{name}", a.shape, mybir.dt.from_np(a.dtype), kind="ExternalInput").ap())
    out = nc.dram_tensor("out", (B * S, P), F32, kind="ExternalOutput").ap()
    build(nc, *args, out)
    r = _run(nc, [arrays], core_ids=[0])
    return r.results[0]["out"].reshape(B, S, P)
```
